# Optimizing a Trainium2 kernel written in Bass

```python
import numpy as np
import jax
import jax.numpy as jnp

def _softmax(x, axis=-1):
    return jax.nn.softmax(x, axis=axis)

def _gelu(x):
    return jax.nn.gelu(x, approximate=True)

def _silu(x):
    return jax.nn.silu(x)

def _sigmoid(x):
    return jax.nn.sigmoid(x)

def _layernorm(x, axis=-1, eps=1e-05):
    m = jnp.mean(x, axis=axis, keepdims=True)
    v = jnp.var(x, axis=axis, keepdims=True)
    return (x - m) / jnp.sqrt(v + eps)

def _scatter_add(tgt, idx, src, axis=0):
    return tgt.at[idx].add(src)

def _segment_sum(src, seg, n):
    return jax.ops.segment_sum(src, seg, n)
kernel_name = 'mk_gnn_ffn_d1_gnn_r8_8c3cd7'

def setup_inputs(seed: int=0):
    np.random.seed(seed)
    _w = jnp.asarray

    def _rec_inputs():
        import jax
        import jax.numpy as jnp
        _gk = jax.random.key(seed)
        x = -6.415e-05 + 1 * jax.random.normal(jax.random.fold_in(_gk, 1), (6250, 256), jnp.float32)
        _s = jax.random.randint(jax.random.fold_in(_gk, 2), (50000,), 0, 6250, jnp.int32)
        _d = jax.random.randint(jax.random.fold_in(_gk, 3), (50000,), 0, 6250, jnp.int32)
        _loop = jnp.arange(6250, dtype=jnp.int32)
        src = jnp.concatenate([_s, _d, _loop])
        dst = jnp.concatenate([_d, _s, _loop])
        _o = jnp.argsort(dst, stable=True)
        src = src[_o]
        dst = dst[_o]
        edge_type_8 = jax.random.randint(jax.random.fold_in(_gk, 12), (106250,), 0, 8, jnp.int32)
        edge_weight = jax.random.uniform(jax.random.fold_in(_gk, 13), (106250,), jnp.float32, 0.0, 1)
        return (x, src, dst, edge_type_8, edge_weight)
    x, src, dst, edge_type_8, edge_weight = _rec_inputs()

    def _L0_gnn_setup():
        import jax, jax.numpy as jnp
        import numpy as np
        N_NODES = 5000
        N_EDGES = 80000
        IN_FEAT = 256
        OUT_FEAT = 256
        NUM_RELS = 8
        key = jax.random.key(seed)
        k = jax.random.split(key, 6)
        h = jax.random.normal(k[0], (N_NODES, IN_FEAT), dtype=jnp.float32)
        norm = jax.random.uniform(k[1], (N_EDGES,), dtype=jnp.float32)
        gain = float(np.sqrt(2.0))
        bound = gain * float(np.sqrt(6.0 / (IN_FEAT + OUT_FEAT)))
        weight = jax.random.uniform(k[2], (NUM_RELS, IN_FEAT, OUT_FEAT), dtype=jnp.float32, minval=-bound, maxval=bound)
        edge_src = jax.random.randint(k[3], (N_EDGES,), 0, N_NODES)
        edge_dst = jax.random.randint(k[4], (N_EDGES,), 0, N_NODES)
        edge_type = jax.random.randint(k[5], (N_EDGES,), 0, NUM_RELS)
        return {'h': h, 'norm': norm, 'weight': weight, 'edge_src': edge_src, 'edge_dst': edge_dst, 'edge_type': edge_type}
    _L0_gnn_all = _L0_gnn_setup()
    _L0_gnn_in = {k: v for k, v in _L0_gnn_all.items() if k in ('weight',)}
    del _L0_gnn_all

    def _L0_ffn_setup():
        import jax, jax.numpy as jnp
        import numpy as np
        BN_EPS = 0.001

        def _bn(h, g, b, m, v):
            return g * (h - m) * jax.lax.rsqrt(v + BN_EPS) + b
        key = jax.random.key(seed)
        ks = jax.random.split(key, 8)
        B, F, Df = (256, 64, 256)
        E, H, D = (8, 256, 256)
        s1 = 1.0 / np.sqrt(Df)
        s2 = 1.0 / np.sqrt(H)
        return {'x': jax.random.normal(ks[0], (B, F, Df), jnp.float32), 'Wr': jax.random.normal(ks[1], (Df, E), jnp.float32) * s1, 'br': jnp.zeros((E,), jnp.float32), 'W1': jax.random.normal(ks[2], (E, Df, H), jnp.float32) * s1, 'b1': jnp.zeros((E, H), jnp.float32), 'g1': jnp.ones((E, H), jnp.float32), 'be1': jnp.zeros((E, H), jnp.float32), 'm1': jnp.zeros((E, H), jnp.float32), 'v1': jnp.ones((E, H), jnp.float32), 'W2': jax.random.normal(ks[3], (E, H, H), jnp.float32) * s2, 'b2': jnp.zeros((E, H), jnp.float32), 'g2': jnp.ones((E, H), jnp.float32), 'be2': jnp.zeros((E, H), jnp.float32), 'm2': jnp.zeros((E, H), jnp.float32), 'v2': jnp.ones((E, H), jnp.float32), 'Wo': jax.random.normal(ks[4], (E, H, D), jnp.float32) * s2, 'bo': jnp.zeros((E, D), jnp.float32)}
    _L0_ffn_all = _L0_ffn_setup()
    _L0_ffn_in = {k: v for k, v in _L0_ffn_all.items() if k in ('Wr', 'br', 'W1', 'b1', 'g1', 'be1', 'm1', 'v1', 'W2', 'b2', 'g2', 'be2', 'm2', 'v2', 'Wo', 'bo')}
    del _L0_ffn_all
    return {'x': x, 'src': src, 'dst': dst, 'edge_type_8': edge_type_8, 'edge_weight': edge_weight, 'L0_gnn_weight': _L0_gnn_in['weight'], 'L0_ffn_Wr': _L0_ffn_in['Wr'], 'L0_ffn_br': _L0_ffn_in['br'], 'L0_ffn_W1': _L0_ffn_in['W1'], 'L0_ffn_b1': _L0_ffn_in['b1'], 'L0_ffn_g1': _L0_ffn_in['g1'], 'L0_ffn_be1': _L0_ffn_in['be1'], 'L0_ffn_m1': _L0_ffn_in['m1'], 'L0_ffn_v1': _L0_ffn_in['v1'], 'L0_ffn_W2': _L0_ffn_in['W2'], 'L0_ffn_b2': _L0_ffn_in['b2'], 'L0_ffn_g2': _L0_ffn_in['g2'], 'L0_ffn_be2': _L0_ffn_in['be2'], 'L0_ffn_m2': _L0_ffn_in['m2'], 'L0_ffn_v2': _L0_ffn_in['v2'], 'L0_ffn_Wo': _L0_ffn_in['Wo'], 'L0_ffn_bo': _L0_ffn_in['bo']}

def reference(x, src, dst, edge_type_8, edge_weight, L0_gnn_weight, L0_ffn_Wr, L0_ffn_br, L0_ffn_W1, L0_ffn_b1, L0_ffn_g1, L0_ffn_be1, L0_ffn_m1, L0_ffn_v1, L0_ffn_W2, L0_ffn_b2, L0_ffn_g2, L0_ffn_be2, L0_ffn_m2, L0_ffn_v2, L0_ffn_Wo, L0_ffn_bo):
    import jax
    import jax.numpy as jnp

    def _L0_gnn_ref(h, norm, weight, edge_src, edge_dst, edge_type):
        import jax, jax.numpy as jnp
        import numpy as np
        N_NODES = 5000
        N_EDGES = 80000
        IN_FEAT = 256
        OUT_FEAT = 256
        NUM_RELS = 8
        transformed = jnp.einsum('ni,rio->rno', h, weight)
        msg = transformed[edge_type, edge_src] * norm[:, None]
        agg = jax.ops.segment_sum(msg, edge_dst, num_segments=h.shape[0])
        return jax.nn.relu(agg)

    def _L0_ffn_ref(x, Wr, br, W1, b1, g1, be1, m1, v1, W2, b2, g2, be2, m2, v2, Wo, bo):
        import jax, jax.numpy as jnp
        import numpy as np
        BN_EPS = 0.001

        def _bn(h, g, b, m, v):
            return g * (h - m) * jax.lax.rsqrt(v + BN_EPS) + b
        feat = jnp.mean(x, axis=0)
        w = jax.nn.softmax(feat @ Wr + br, axis=-1)
        h = jnp.einsum('bfd,edh->bfeh', x, W1) + b1
        h = jax.nn.relu(_bn(h, g1, be1, m1, v1))
        h = jnp.einsum('bfeh,ehk->bfek', h, W2) + b2
        h = jax.nn.relu(_bn(h, g2, be2, m2, v2))
        y = jnp.einsum('bfeh,ehd->bfed', h, Wo) + bo
        return jnp.einsum('bfed,fe->bfd', y, w)
    x = x + _L0_gnn_ref(_layernorm(x, axis=-1), edge_weight, L0_gnn_weight, src, dst, edge_type_8)
    x = x + _L0_ffn_ref(_layernorm(x, axis=-1)[None], L0_ffn_Wr, L0_ffn_br, L0_ffn_W1, L0_ffn_b1, L0_ffn_g1, L0_ffn_be1, L0_ffn_m1, L0_ffn_v1, L0_ffn_W2, L0_ffn_b2, L0_ffn_g2, L0_ffn_be2, L0_ffn_m2, L0_ffn_v2, L0_ffn_Wo, L0_ffn_bo)[0]
    return x

_drawn_inputs = setup_inputs


def setup_inputs(seed=0):
    import zlib

    import numpy as np

    out = dict(_drawn_inputs(seed))
    spreads = {'L0_ffn_br': (0.0, 0.6),
     'L0_ffn_b1': (0.0, 0.8),
     'L0_ffn_g1': (1.0, 0.6),
     'L0_ffn_be1': (0.0, 0.8),
     'L0_ffn_m1': (0.0, 0.8),
     'L0_ffn_v1': (1.0, 0.6),
     'L0_ffn_b2': (0.0, 0.575),
     'L0_ffn_g2': (1.0, 0.6),
     'L0_ffn_be2': (0.0, 0.602),
     'L0_ffn_m2': (0.0, 0.594),
     'L0_ffn_v2': (1.0, 0.6),
     'L0_ffn_bo': (0.0, 0.43)}
    factors = {}
    for name, (base, spread) in spreads.items():
        noise = np.random.default_rng([zlib.crc32(name.encode()), seed]).standard_normal(out[name].shape)
        drawn = base * np.exp(spread * noise) if base else spread * noise
        out[name] = jnp.asarray(drawn.astype(out[name].dtype))
    for name, factor in factors.items():
        out[name] = (out[name] * factor).astype(out[name].dtype)
    return out
```

```python
import concourse.bass as bass
from concourse import mybir
from contextlib import ExitStack

N = 6250
D = 256
E = 106250
R = 8
X = 8
KH = D // 128
P = 128
BN_EPS = 0.001
LN_EPS = 1e-5

GT = 3
GE = GT * P
NG = -(-E // GE)
W = 32
CH = 3
CG = -(-NG // CH)
COLS = CH * CG * GT

QT = 3
BT = QT * P
HEAD = N % BT
NBLK = N // BT
GB = 17
LEAD = 7
PRO = 12
JP = LEAD + GB - PRO
READ = 5
BIAS = 3
LAST = NBLK
WS = 256
NW = -(-N // WS)
NP = NW * WS

EARLY = 4
SLOTS = 13
SS = 6


def groups_of(t):
    return max(0, min(GB, NG - PRO - GB * t))


def lower_bounds():
    import numpy as np
    g = np.arange(CH * CG)
    low = np.where(g >= LEAD, HEAD + BT * ((g - LEAD) // GB), 0)
    low = np.where(g < NG, np.minimum(low, N), 0)
    return np.ascontiguousarray(low.reshape(CH, CG).T.astype(np.float32))


def gnn_ffn(nc, x, src, dst, etype, weight_e, wg, wr, br, w1, b1, g1, be1, m1, v1,
            w2, b2, g2, be2, m2, v2, wo, bo, low, out):
    dt = mybir.dt
    f32, f32r, f16, i32 = dt.float32, dt.float32r, dt.float16, dt.int32
    ALU, ACT, AX = mybir.AluOpType, mybir.ActivationFunctionType, mybir.AxisListType
    ds = bass.ds

    table = nc.dram_tensor("messages_table", [N * R, 2 * D], f16).ap()

    nodes = nc.dram_tensor("edge_nodes", [P, COLS], f32).ap()

    keep = ExitStack()
    with keep:
        def sb(name, shape, d, ctx=keep):
            return ctx.enter_context(nc.sbuf_tensor(name, shape, d))

        def sem(name, ctx=keep):
            return ctx.enter_context(nc.semaphore(name))

        W1h, W1l = sb("W1h", [P, X, KH, D], f32r), sb("W1l", [P, X, KH, D], f32r)
        W2h, W2l = sb("W2h", [P, X, KH, D], f32r), sb("W2l", [P, X, KH, D], f32r)
        Woh, Wol = sb("Woh", [P, X, KH, D], f32r), sb("Wol", [P, X, KH, D], f32r)
        Wrh, Wrl = sb("Wrh", [P, KH, X], f32r), sb("Wrl", [P, KH, X], f32r)
        bo24 = sb("bo24", [3 * X, D], f32r)
        brb = sb("brb", [P, X], f32)
        ident = sb("ident", [P, P], f32)
        iota2 = sb("iota2", [P, 2, W], f16)
        eps = sb("eps", [P, 1], f32)
        bnp = sb("bnp", [P, 4, 2 * X], f32)
        idx = sb("idx", [P, COLS], i32)
        rel = sb("rel", [P, COLS], f32)
        wp = sb("wp", [P, COLS, 2], f16)
        base = sb("base", [1, CH * CG], i32)
        bad = sb("bad", [1, 1], i32)

        s_table = sem("table_stored")

        A = ExitStack()
        with A:
            node = sb("node", [P, COLS], f32, A)
            Wgh, Wgl = sb("Wgh", [P, KH, R, D], f32r, A), sb("Wgl", [P, KH, R, D], f32r, A)
            NWS = 2
            wraw = sb("wraw", [P, NWS, KH, D], f32, A)
            fraw = sb("fraw", [P, 2, KH, D], f32, A)
            xin = sb("xin", [P, 2, D], f32, A)
            xn = sb("xn", [P, 2, D], f32, A)
            xTh, xTl = sb("xTh", [P, 2, KH, P], f32r, A), sb("xTl", [P, 2, KH, P], f32r, A)
            stage = sb("stage", [P, 2, R, 2 * D], f16, A)
            st6, mv, sd = sb("st6", [P, 6], f32, A), sb("mv", [P, 2], f32, A), sb("sd", [P, 2], f32, A)
            e_src, e_dst = sb("e_src", [CG, CH, GE], i32, A), sb("e_dst", [CG, CH, GE], i32, A)
            e_typ, e_w = sb("e_typ", [CG, CH, GE], i32, A), sb("e_w", [CG, CH, GE], f32, A)
            e_row = e_src[:, :, :].bitcast(f32)
            e_node = sb("e_node", [CG, CH, GE], f32, A)
            e_rel = e_dst[:, :, :].bitcast(f32)
            gmin, gmax = sb("gmin", [CG, CH], f32, A), sb("gmax", [CG, CH], f32, A)
            lowt, viol = sb("lowt", [CG, CH], f32, A), sb("viol", [CG, 2, CH], f32, A)
            vio2 = sb("vio2", [CG, 2], f32, A)
            ones = sb("ones", [P, P], f32, A)
            praw = sb("praw", [2 * X, 10, P], f32, A)
            wrr = sb("wrr", [P, KH, X], f32, A)
            bor = sb("bor", [X, D], f32, A)
            boh, bol = sb("boh", [X, D], f32r, A), sb("bol", [X, D], f32r, A)
            psT = [A.enter_context(nc.psum_tensor(f"psT{i}", [P, KH, P], f32)) for i in range(1)]
            psP = [A.enter_context(nc.psum_tensor(f"psP{i}", [P, 2, D], f32)) for i in range(4)]
            psE = A.enter_context(nc.psum_tensor("psE", [P, 512], f32))

            s_eps, s_wpad = sem("eps_set", A), sem("weight_padding_zero", A)
            s_edge, s_par = sem("edges_loaded", A), sem("params_loaded", A)
            s_wgl = [sem(f"wg_loaded{i}", A) for i in range(NWS)]
            s_wgh, s_wgd = sem("wg_high", A), sem("wg_split", A)
            s_x = [sem(f"x_loaded{i}", A) for i in range(2)]
            s_ln, s_sd, s_xn = sem("ln_chain", A), sem("deviation", A), sem("x_normed", A)
            s_tr, s_xh, s_xl = sem("x_transposed", A), sem("xT_high", A), sem("xT_low", A)
            s_mm, s_th, s_tl = sem("messages_done", A), sem("table_high", A), sem("table_low", A)
            s_st = [sem(f"stage_stored{i}", A) for i in range(2)]
            s_nd = sem("nodes_stored", A)
            s_node, s_el = sem("edge_nodes", A), sem("edge_chain", A)
            s_p, s_ep = sem("pool_chain", A), sem("edges_prepared", A)
            s_bn, s_bs = sem("bn_chain", A), sem("bn_root", A)
            s_et, s_ee = sem("edge_transposed", A), sem("edge_evacuated", A)
            s_fl = [sem(f"ffn_loaded{i}", A) for i in range(2)]
            s_fd = sem("ffn_split", A)
            s_wh = sem("edge_weight_high", A)
            s_bo, s_bom = sem("bo_split", A), sem("bo_placed", A)

            NT = -(-N // P)
            TAIL = N - (NT - 1) * P
            PAIRS = R // 2
            FULL = NG - 1 - (CH - 1) * CG
            PADS = CG - FULL - 1
            NEDGE = 3 * (CH + 2 + PADS) + (CH + 1) + 1
            NPAR = 13
            ffn = [(hi, lo, a, e) for hi, lo, a in ((W1h, W1l, w1), (W2h, W2l, w2), (Woh, Wol, wo)) for e in range(X)]
            edge_jobs = [(q, c) for q in range(4) for c in range(CH)]
            NJ = len(edge_jobs)

            with nc.Block() as block:
                @block.sync
                def _(sp):
                    for s in range(2):
                        sp.dma_start(xin[:, s, :], x[s * P:(s + 1) * P, :]).then_inc(s_x[s], 16)
                    o = (CH - 1) * CG * GE
                    left = E - o - FULL * GE
                    for tile, a in ((e_dst, dst), (e_src, src), (e_typ, etype), (e_w, weight_e)):
                        for c in range(CH - 1):
                            sp.dma_start(tile[:, c, :], a[c * CG * GE:(c + 1) * CG * GE]
                                         .rearrange("(g k) -> g k", k=GE)).then_inc(s_edge, 16)
                        if tile is e_w:
                            sp.wait_ge(s_wpad, 1)
                        sp.dma_start(tile[0:FULL, CH - 1, :], a[o:o + FULL * GE]
                                     .rearrange("(g k) -> g k", k=GE)).then_inc(s_edge, 16)
                        sp.dma_start(tile[FULL:FULL + 1, CH - 1, 0:left],
                                     a[E - left:E].rearrange("(g k) -> g k", k=left)).then_inc(s_edge, 16)
                        if tile is not e_w:
                            sp.dma_start(tile[FULL:FULL + 1, CH - 1, left:GE],
                                         a[E - GE + left:E].rearrange("(g k) -> g k", k=GE - left)).then_inc(s_edge, 16)
                            for g in range(FULL + 1, CG):
                                sp.dma_start(tile[g:g + 1, CH - 1, :],
                                             a[E - GE:E].rearrange("(g k) -> g k", k=GE)).then_inc(s_edge, 16)
                    sp.dma_start(lowt[:, :], low).then_inc(s_edge, 16)

                    def tile_io(t, s, more):
                        sp.wait_ge(s_xn, t + 1)
                        if more == P:
                            sp.dma_start(xin[:, s, :], x[ds((t + 2) * P, P), :]).then_inc(s_x[s], 16)
                        elif more:
                            sp.dma_start(xin[0:more, s, :], x[N - more:N, :]).then_inc(s_x[s], 16)
                        sp.wait_ge(s_tl, PAIRS * (t + 1))
                        sp.dma_start(table[ds(t * P * R, P * R), :].rearrange("(p r) c -> p (r c)", r=R),
                                     stage[:, s, :, :].rearrange("p r c -> p (r c)")).then_inc(s_st[s], 16)

                    with sp.Fori(0, NT // 2 - 1) as i:
                        for s in range(2):
                            tile_io(2 * i + s, s, P)
                    tile_io(NT - 3, 0, TAIL)
                    tile_io(NT - 2, 1, 0)
                    sp.wait_ge(s_tl, PAIRS * NT)
                    sp.dma_start(table[(NT - 1) * P * R:N * R, :].rearrange("(p r) c -> p (r c)", r=R),
                                 stage[0:TAIL, 0, :, :].rearrange("p r c -> p (r c)")).then_inc(s_st[0], 16)
                    sp.wait_ge(s_bo, 2)
                    for k, part in enumerate((boh, boh, bol)):
                        sp.dma_start(bo24[k * X:(k + 1) * X, :].bitcast(f32), part[:, :].bitcast(f32)).then_inc(s_bom, 16)
                    sp.wait_ge(s_bom, 48)
                    sp.wait_ge(s_ee, NJ)
                    sp.dma_start(nodes, node[:, :]).then_inc(s_nd, 16)
                    sp.wait_ge(s_nd, 16)
                    sp.wait_ge(s_st[0], 16 * (NT // 2 + 1))
                    sp.wait_ge(s_st[1], 16 * (NT // 2))

                @block.scalar
                def _(act):
                    def load_wg(r):
                        act.dma_start(wraw[:, r % NWS, :, :], wg[r, :, :].rearrange("(k p) n -> p k n", p=P))\
                           .then_inc(s_wgl[r % NWS], 16)

                    for r in range(NWS):
                        load_wg(r)
                    for a, j in ((g1, 0), (v1, 1), (b1, 2), (m1, 3), (be1, 4),
                                 (g2, 5), (v2, 6), (b2, 7), (m2, 8), (be2, 9)):
                        act.dma_start(praw[:, j, :], a.rearrange("e (h p) -> (e h) p", p=P)).then_inc(s_par, 16)
                    act.dma_start(wrr[:, :, :], wr.rearrange("(k p) n -> p k n", p=P)).then_inc(s_par, 16)
                    act.dma_start(bor[:, :], bo).then_inc(s_par, 16)
                    act.dma_start(brb[:, :], br.rearrange("(a n) -> a n", a=1).to_broadcast([P, X])).then_inc(s_par, 16)

                    def deviation(t):
                        act.wait_ge(s_ln, 4 * t + 3)
                        nc.scalar.activation(sd[:, 0:1], mv[:, 1:2], ACT.Sqrt, bias=eps[:, 0:1]).then_inc(s_sd, 1)

                    def xT_high(t, s, rows):
                        act.wait_ge(s_tr, t + 1)
                        nc.scalar.copy(xTh[:, s, :, 0:rows], psT[0][:, :, 0:rows]).then_inc(s_xh, 1)

                    def t_high(t, s, k, rows, stored):
                        act.wait_ge(s_mm, PAIRS * t + k + 1)
                        if k == 0 and stored is not None:
                            act.wait_ge(s_st[s], 16 * stored)
                        nc.scalar.copy(stage[0:rows, s, 2 * k:2 * k + 2, 0:D], psP[k][0:rows, :, :]).then_inc(s_th, 1)

                    def tile(t, s, rows_next, stored):
                        deviation(t + 1)
                        for k in range(PAIRS):
                            t_high(t, s, k, P, stored)
                            if k == 1:
                                xT_high(t + 1, 1 - s, rows_next)

                    deviation(0)
                    for r in range(R):
                        act.wait_ge(s_wgl[r % NWS], 16 * (r // NWS + 1))
                        nc.scalar.copy(Wgh[:, :, r, :], wraw[:, r % NWS, :, :]).then_inc(s_wgh, 1)
                        if r == 0:
                            xT_high(0, 0, P)
                        if r + NWS < R:
                            act.wait_ge(s_wgd, r + 1)
                            load_wg(r + NWS)
                    tile(0, 0, P, None)
                    tile(1, 1, P, None)
                    with act.Fori(1, EARLY) as i:
                        for s in range(2):
                            tile(2 * i + s, s, P, i)
                    act.wait_ge(s_bn, 2)
                    nc.scalar.activation(praw[:, 1, :], praw[:, 1, :], ACT.Sqrt)
                    nc.scalar.activation(praw[:, 6, :], praw[:, 6, :], ACT.Sqrt).then_inc(s_bs, 1)
                    for n, (q, c) in enumerate(edge_jobs):
                        act.wait_ge(s_et, n + 1)
                        lot = (idx[:, :], rel[:, :], wp[:, :, 0], node[:, :])[q]
                        nc.scalar.copy(lot[:, GT * CG * c:GT * CG * (c + 1)].rearrange("p (g i) -> p i g", i=GT),
                                       psE[:, 0:GT * CG].rearrange("p (i g) -> p i g", i=GT))\
                            .then_inc(s_wh if q == 2 else s_ee, 1)
                    act.wait_ge(s_et, NJ + 1)
                    nc.scalar.copy(base[0:1, :], psE[0:1, 0:CH * CG]).then_inc(s_ee, 1)
                    act.wait_ge(s_et, NJ + 2)
                    nc.scalar.copy(bnp[:, :, :], psE[:, 0:8 * X].rearrange("p (q c) -> p q c", q=4)).then_inc(s_ee, 1)
                    with act.Fori(EARLY, NT // 2 - 1) as i:
                        for s in range(2):
                            tile(2 * i + s, s, P, i)
                    tile(NT - 3, 0, P, NT // 2 - 1)
                    tile(NT - 2, 1, TAIL, NT // 2 - 1)
                    for k in range(PAIRS):
                        t_high(NT - 1, 0, k, TAIL, NT // 2)

                @block.vector
                def _(dve):
                    dve.memset(eps[:, :], LN_EPS).then_inc(s_eps, 1)

                    def norm(t, s, c, rows):
                        dve.wait_ge(s_x[s], 16 * (c + 1))
                        dve.bn_stats(st6[0:rows, :], xin[0:rows, s, :]).then_inc(s_ln, 1)
                        dve.wait_ge(s_ln, 4 * t + 1)
                        dve.sem_inc(s_ln, 1)
                        dve.bn_aggr(mv[0:rows, :], st6[0:rows, :]).then_inc(s_ln, 1)
                        dve.wait_ge(s_sd, t + 1)
                        dve.reciprocal(sd[0:rows, 1:2], sd[0:rows, 0:1]).then_inc(s_ln, 1)
                        dve.wait_ge(s_ln, 4 * t + 4)
                        dve.tensor_scalar(xn[0:rows, s, :], xin[0:rows, s, :], mv[0:rows, 0:1], sd[0:rows, 1:2],
                                          ALU.subtract, ALU.mult).then_inc(s_xn, 1)

                    def xT_low(t, s, rows):
                        dve.wait_ge(s_xh, t + 1)
                        dve.tensor_tensor(xTl[:, s, :, 0:rows], psT[0][:, :, 0:rows], xTh[:, s, :, 0:rows],
                                          ALU.subtract).then_inc(s_xl, 1)

                    def t_low(t, s, k, rows):
                        dve.wait_ge(s_th, PAIRS * t + k + 1)
                        dve.tensor_tensor(stage[0:rows, s, 2 * k:2 * k + 2, D:2 * D], psP[k][0:rows, :, :],
                                          stage[0:rows, s, 2 * k:2 * k + 2, 0:D], ALU.subtract).then_inc(s_tl, 1)

                    def tile(t, s, c_next, rows_next):
                        norm(t + 1, 1 - s, c_next, rows_next)
                        for k in range(PAIRS):
                            t_low(t, s, k, P)
                            if k == 1:
                                xT_low(t + 1, 1 - s, rows_next)

                    dve.wait_ge(s_eps, 1)
                    dve.memset(mv[:, :], 0.0).then_inc(s_eps, 1)
                    dve.wait_ge(s_eps, 2)
                    norm(0, 0, 0, P)
                    for r in range(R):
                        dve.wait_ge(s_wgh, r + 1)
                        dve.tensor_tensor(Wgl[:, :, r, :], wraw[:, r % NWS, :, :], Wgh[:, :, r, :], ALU.subtract)\
                           .then_inc(s_wgd, 1)
                        if r == 0:
                            xT_low(0, 0, P)
                    tile(0, 0, 0, P)
                    tile(1, 1, 1, P)
                    with dve.Fori(1, EARLY) as i:
                        for s in range(2):
                            tile(2 * i + s, s, i + s, P)
                    n = [0]

                    def edge_link(ins):
                        n[0] += 1
                        ins.then_inc(s_el, 1)
                        dve.wait_ge(s_el, n[0])

                    dve.wait_ge(s_node, 1)
                    edge_link(dve.tensor_reduce(gmax[:, :], e_node[:, :, :], AX.X, ALU.max))
                    edge_link(dve.tensor_reduce(gmin[:, :], e_node[:, :, :], AX.X, ALU.min))
                    edge_link(dve.tensor_tensor(viol[:, 0, :], gmax[:, :], gmin[:, :], ALU.subtract))
                    edge_link(dve.tensor_scalar(viol[:, 0, :], viol[:, 0, :], W - 0.5, None, ALU.is_gt))
                    edge_link(dve.tensor_tensor(viol[:, 1, :], gmin[:, :], lowt[:, :], ALU.is_lt))
                    edge_link(dve.tensor_tensor(viol[:, 0, :], viol[:, 0, :], viol[:, 1, :], ALU.add))
                    edge_link(dve.tensor_reduce(vio2[:, 0:1], viol[:, 0, :], AX.X, ALU.add))
                    edge_link(dve.tensor_copy(vio2[:, 1:2], vio2[:, 0:1]))
                    for c in range(CH):
                        last = dve.tensor_scalar(e_rel[:, c, :], e_node[:, c, :], gmin[:, c:c + 1], None,
                                                 ALU.subtract)
                    last.then_inc(s_ep, 1)
                    n = [0]

                    def link(ins):
                        n[0] += 1
                        ins.then_inc(s_bn, 1)
                        dve.wait_ge(s_bn, n[0])

                    dve.wait_ge(s_par, 16 * NPAR)
                    link(dve.tensor_scalar(praw[:, 1, :], praw[:, 1, :], BN_EPS, None, ALU.add))
                    link(dve.tensor_scalar(praw[:, 6, :], praw[:, 6, :], BN_EPS, None, ALU.add))
                    dve.wait_ge(s_bs, 1)
                    for l in range(2):
                        g, v, b, m, be = (praw[:, 5 * l + k, :] for k in range(5))
                        link(dve.reciprocal(v, v))
                        link(dve.tensor_tensor(g, g, v, ALU.mult))
                        link(dve.tensor_tensor(b, b, m, ALU.subtract))
                        link(dve.tensor_tensor(b, b, g, ALU.mult))
                        link(dve.tensor_tensor(b, b, be, ALU.add))
                    for c in range(CH):
                        dve.wait_ge(s_wh, c + 1)
                        part = slice(GT * CG * c, GT * CG * (c + 1))
                        dve.tensor_tensor(wp[:, part, 1].rearrange("p (g i) -> p i g", i=GT),
                                          psE[:, 0:GT * CG].rearrange("p (i g) -> p i g", i=GT),
                                          wp[:, part, 0].rearrange("p (g i) -> p i g", i=GT), ALU.subtract)\
                           .then_inc(s_ee, 1)
                    dve.wait_ge(s_et, NJ + 3)
                    dve.tensor_scalar(bad[0:1, 0:1], psE[0:1, 0:1], 0.5, None, ALU.is_gt).then_inc(s_ee, 1)
                    with dve.Fori(EARLY, NT // 2 - 1) as i:
                        for s in range(2):
                            tile(2 * i + s, s, i + s, P)
                    tile(NT - 3, 0, NT // 2 - 1, P)
                    tile(NT - 2, 1, NT // 2, TAIL)
                    for k in range(PAIRS):
                        t_low(NT - 1, 0, k, TAIL)

                @block.gpsimd
                def _(pool):
                    n = [0]

                    def link(ins):
                        n[0] += 1
                        ins.then_inc(s_p, 1)
                        pool.wait_ge(s_p, n[0])

                    link(nc.gpsimd.memset(ident[:, :], 0.0))
                    link(nc.gpsimd.affine_select(out=ident[:, :], in_=ident[:, :], compare_op=ALU.not_equal, fill=1.0,
                                                 base=0, pattern=[[-1, P]], channel_multiplier=1))
                    nc.gpsimd.memset(e_w[:, CH - 1, :], 0.0).then_inc(s_wpad, 1)
                    nc.gpsimd.memset(ones[:, :], 1.0)
                    nc.gpsimd.iota(iota2[:, :, :], pattern=[[0, 2], [1, W]], base=0, channel_multiplier=0,
                                   allow_small_or_imprecise_dtypes=True)
                    pool.wait_ge(s_edge, 16 * NEDGE)
                    link(nc.gpsimd.tensor_scalar(e_row[:, :, :], e_src[:, :, :], float(R), None, ALU.mult))
                    link(nc.gpsimd.tensor_copy(e_node[:, :, :], e_typ[:, :, :]))
                    link(nc.gpsimd.tensor_tensor(e_row[:, :, :], e_row[:, :, :], e_node[:, :, :], ALU.add))
                    nc.gpsimd.tensor_copy(e_node[:, :, :], e_dst[:, :, :]).then_inc(s_node, 1)
                    pool.wait_ge(s_par, 16 * NPAR)
                    nc.gpsimd.tensor_copy(boh[:, :], bor[:, :]).then_inc(s_bo, 1)
                    link(nc.gpsimd.tensor_copy(Wrh[:, :, :], wrr[:, :, :]))
                    nc.gpsimd.tensor_tensor(Wrl[:, :, :], wrr[:, :, :], Wrh[:, :, :], ALU.subtract)
                    pool.wait_ge(s_bo, 1)
                    nc.gpsimd.tensor_tensor(bol[:, :], bor[:, :], boh[:, :], ALU.subtract).then_inc(s_bo, 1)

                    def load(j):
                        _, _, a, e = ffn[j]
                        pool.dma_start(fraw[:, j % 2, :, :], a[e, :, :].rearrange("(k p) n -> p k n", p=P))\
                            .then_inc(s_fl[j % 2], 16)

                    load(0)
                    for j, (hi, lo, _, e) in enumerate(ffn):
                        if j + 1 < len(ffn):
                            if j >= 1:
                                pool.wait_ge(s_fd, 2 * j)
                            load(j + 1)
                        pool.wait_ge(s_fl[j % 2], 16 * (j // 2 + 1))
                        nc.gpsimd.tensor_copy(hi[:, e, :, :], fraw[:, j % 2, :, :]).then_inc(s_fd, 1)
                        pool.wait_ge(s_fd, 2 * j + 1)
                        nc.gpsimd.tensor_tensor(lo[:, e, :, :], fraw[:, j % 2, :, :], hi[:, e, :, :],
                                                ALU.subtract).then_inc(s_fd, 1)

                @block.tensor
                def _(pe):
                    def transpose_x(t, s, rows):
                        pe.wait_ge(s_xn, t + 1)
                        if not (isinstance(t, int) and t == 0):
                            pe.wait_ge(s_xl, t)
                        for h in range(KH):
                            last = nc.tensor.transpose(psT[0][:, h, 0:rows], xn[0:rows, s, h * P:(h + 1) * P],
                                                       ident[0:rows, 0:rows])
                        last.then_inc(s_tr, 1)

                    def messages(t, s, k, rows):
                        if k == 0:
                            pe.wait_ge(s_xl, t + 1)
                        if isinstance(t, int) and t == 0:
                            pe.wait_ge(s_wgd, 2 * k + 2)
                        else:
                            pe.wait_ge(s_tl, PAIRS * t + k - 3)
                        n = 0
                        for h in range(KH):
                            for a, b in ((xTh, Wgh), (xTh, Wgl), (xTl, Wgh)):
                                last = nc.tensor.matmul(psP[k][0:rows, :, :], a[:, s, h, 0:rows], b[:, h, 2 * k:2 * k + 2, :],
                                                        start=(n == 0), stop=(n == 5))
                                n += 1
                        last.then_inc(s_mm, 1)

                    def tile(t, s, rows_next):
                        for k in range(PAIRS):
                            messages(t, s, k, P)
                            if k == 1:
                                transpose_x(t + 1, 1 - s, rows_next)

                    pe.wait_ge(s_p, 2)
                    transpose_x(0, 0, P)
                    tile(0, 0, P)
                    tile(1, 1, P)
                    with pe.Fori(1, EARLY) as i:
                        for s in range(2):
                            tile(2 * i + s, s, P)
                    pe.wait_ge(s_ep, 1)
                    for n, (q, c) in enumerate(edge_jobs):
                        if n:
                            pe.wait_ge(s_ee, n)
                        part = (e_row, e_rel, e_w, e_node)[q]
                        for i in range(GT):
                            last = nc.tensor.transpose(psE[:, CG * i:CG * (i + 1)], part[:, c, i * P:(i + 1) * P],
                                                       ident[0:CG, 0:CG])
                        last.then_inc(s_et, 1)
                    pe.wait_ge(s_ee, NJ)
                    for c in range(CH):
                        last = nc.tensor.transpose(psE[0:1, CG * c:CG * (c + 1)], gmin[:, c:c + 1], ident[0:CG, 0:CG])
                    last.then_inc(s_et, 1)
                    pe.wait_ge(s_ee, NJ + 1)
                    pe.wait_ge(s_bn, 12)
                    for q in range(4):
                        last = nc.tensor.transpose(psE[:, 2 * X * q:2 * X * (q + 1)], praw[:, (0, 2, 5, 7)[q], :], ident[0:2 * X, 0:2 * X])
                    last.then_inc(s_et, 1)
                    pe.wait_ge(s_ee, NJ + 2)
                    nc.tensor.matmul(psE[:, 0:2], ones[0:CG, :], vio2[:, :], start=True, stop=True).then_inc(s_et, 1)
                    pe.wait_ge(s_ee, NJ + 3)
                    with pe.Fori(EARLY, NT // 2 - 1) as i:
                        for s in range(2):
                            tile(2 * i + s, s, P)
                    tile(NT - 3, 0, P)
                    tile(NT - 2, 1, TAIL)
                    for k in range(PAIRS):
                        messages(NT - 1, 0, k, TAIL)

        sumT = sb("sumT", [P, KH, NP], f32)
        B = ExitStack()
        with B:
            rows3, gat3 = sb("rows3", [P, GT], i32, B), sb("gat3", [P, GT, 2 * D], f16, B)
            sel3 = sb("sel3", [P, GT, 2, WS], f16, B)
            iotaW = sb("iotaW", [P, 2, WS], f16, B)
            relw = sb("relw", [P, GT], f32, B)
            nodeB = sb("nodeB", [P, COLS], f32, B)
            psW = [B.enter_context(nc.psum_tensor(f"psW{h}", [P, 2, WS], f32)) for h in range(KH)]
            z_iota, z_clear = sem("wide_iota", B), sem("sums_cleared", B)
            z_node = sem("nodes_loaded", B)
            z_rows, z_gat = sem("rows_staged", B), sem("wide_gathered", B)
            z_sel, z_dve, z_mm = sem("wide_selected", B), sem("wide_chain", B), sem("wide_product", B)

            with nc.Block() as block:
                @block.gpsimd
                def _(pool):
                    nc.gpsimd.iota(iotaW[:, :, :], pattern=[[0, 2], [1, WS]], base=0, channel_multiplier=0,
                                   allow_small_or_imprecise_dtypes=True).then_inc(z_iota, 1)
                    flag = pool.value_load(bad[0:1, 0:1], min_val=0, max_val=1)
                    with pool.If(flag == 1):
                        pool.dma_start(nodeB[:, :], nodes).then_inc(z_node, 16)
                        with pool.Fori(0, NG) as g:
                            pool.wait_ge(z_mm, NW * g + 1)
                            nc.gpsimd.tensor_copy(rows3[:, :], idx[:, ds(GT * g, GT)]).then_inc(z_rows, 1)
                            pool.wait_ge(z_rows, 2 * g + 1)
                            pool.sem_inc(z_rows, 1)
                            for i in range(GT):
                                pool.indirect_dma_start(out=gat3[:, i, :], out_offset=None, in_=table,
                                                        in_offset=bass.IndirectOffsetOnAxis(ap=rows3[:, i:i + 1], axis=0))\
                                    .then_inc(z_gat, 16)

                @block.vector
                def _(dve):
                    dve.memset(sumT[:, :, :], 0.0).then_inc(z_clear, 1)
                    flag = dve.value_load(bad[0:1, 0:1], min_val=0, max_val=1)
                    with dve.If(flag == 1):
                        dve.wait_ge(z_iota, 1)
                        dve.wait_ge(z_clear, 1)
                        dve.wait_ge(z_node, 16)
                        C = 3 * NW + 1
                        with dve.Fori(0, NG) as g:
                            dve.tensor_copy(relw[:, :], nodeB[:, ds(GT * g, GT)]).then_inc(z_dve, 1)
                            with dve.Fori(0, NW) as w:
                                dve.wait_ge(z_dve, C * g + 3 * w + 1)
                                for i in range(GT):
                                    last = dve.scalar_tensor_tensor(
                                        sel3[:, i, :, :], iotaW[:, :, :], relw[:, i:i + 1],
                                        wp[:, ds(GT * g + i, 1), :].rearrange("p a c -> p (a c)").unsqueeze(2)
                                        .to_broadcast([P, 2, WS]), ALU.is_equal, ALU.mult)
                                last.then_inc(z_sel, 1)
                                dve.wait_ge(z_sel, NW * g + w + 1)
                                dve.tensor_scalar(relw[:, :], relw[:, :], float(WS), None, ALU.subtract).then_inc(z_dve, 1)
                                dve.wait_ge(z_mm, NW * g + w + 2)
                                for part in range(2):
                                    if part == 1:
                                        dve.wait_ge(z_dve, C * g + 3 * w + 3)
                                    for h in range(KH):
                                        last = dve.tensor_tensor(sumT[:, h, ds(w * WS, WS)], sumT[:, h, ds(w * WS, WS)],
                                                                 psW[h][:, part, :], ALU.add)
                                    last.then_inc(z_dve, 1)
                        dve.wait_ge(z_dve, C * NG)
                        dve.memset(wp[:, :, :], 0.0)

                @block.tensor
                def _(pe):
                    flag = pe.value_load(bad[0:1, 0:1], min_val=0, max_val=1)
                    with pe.If(flag == 1):
                        pe.sem_inc(z_mm, 1)
                        with pe.Fori(0, NG) as g:
                            with pe.Fori(0, NW) as w:
                                pe.wait_ge(z_gat, 16 * GT * (g + 1))
                                pe.wait_ge(z_sel, NW * g + w + 1)
                                for h in range(KH):
                                    for i in range(GT):
                                        nc.tensor.matmul(psW[h][:, :, :], gat3[:, i, h * P:(h + 1) * P], sel3[:, i, :, :],
                                                         start=(i == 0), stop=False)
                                        last = nc.tensor.matmul(psW[h][:, 0, :], gat3[:, i, D + h * P:D + (h + 1) * P],
                                                                sel3[:, i, 0, :], start=False, stop=(i == GT - 1))
                                last.then_inc(z_mm, 1)

        C = ExitStack()
        with C:
            gat = sb("gat", [P, SLOTS, 2 * D], f16, C)
            sel = sb("sel", [P, SS, GT, 2, W], f16, C)
            HG = (GB + 1) // 2
            rowsA, rowsB = sb("rowsA", [P, GT * HG], i32, C), sb("rowsB", [P, GT * (GB - HG)], i32, C)
            aggT = sb("aggT", [P, KH, BT], f32, C)
            xn2 = aggT[:, :, :].rearrange("p h c -> p (h c)").rearrange("p (q d) -> p q d", d=D)
            x1, acc = sb("x1", [P, QT, D], f32, C), sb("acc", [P, QT, D], f32, C)
            xh, xl = sb("xh", [P, KH, BT], f32r, C), sb("xl", [P, KH, BT], f32r, C)
            act32 = sb("act32", [P, KH, BT], f32, C)
            h1h, h1l = sb("h1h", [P, KH, BT], f32r, C), sb("h1l", [P, KH, BT], f32r, C)
            h2h, h2l = sb("h2h", [P, KH, BT], f32r, C), sb("h2l", [P, KH, BT], f32r, C)
            bst, bmv = sb("bst", [P, QT, 6], f32, C), sb("bmv", [P, QT, 2], f32, C)
            dev, inv = sb("dev", [P, QT, 1], f32, C), sb("inv", [P, QT, 1], f32, C)
            lg, lgm, ex = sb("lg", [P, QT, X], f32, C), sb("lgm", [P, QT, X], f32, C), sb("ex", [P, QT, X], f32, C)
            mx, sm = sb("mx", [P, QT], f32, C), sb("sm", [P, QT], f32, C)
            rw = sb("rw", [P, QT, X], f32, C)
            rw24 = sb("rw24", [P, QT, 3 * X], f32r, C)
            rwT = sb("rwT", [3 * X, QT, P], f32r, C)
            psH = [C.enter_context(nc.psum_tensor(f"psH{i}", [P, 512], f32)) for i in range(4)]
            psY = [C.enter_context(nc.psum_tensor(f"psY{i}", [P, D], f32)) for i in range(2)]
            psA = C.enter_context(nc.psum_tensor("psA", [P, KH, 2, W], f32))
            psM = C.enter_context(nc.psum_tensor("psM", [P, 512], f32))

            c_gat = [sem(f"gathered{i}", C) for i in range(SLOTS)]
            c_freed = sem("slots_freed", C)
            c_rows, c_sel = sem("rows_ready", C), sem("selected", C)
            c_sum, c_add1, c_added = sem("group_product", C), sem("group_added_high", C), sem("group_added", C)
            c_agg = sem("block_sums_read", C)
            c_mm, c_act, c_lo = sem("layer_product", C), sem("activated", C), sem("activation_split", C)
            c_y, c_yd = sem("expert_output", C), sem("output_added", C)
            c_m, c_mr = sem("misc_bank_written", C), sem("misc_bank_read", C)
            c_x, c_out = sem("residual_loaded", C), sem("block_stored", C)
            c_st, c_dev, c_xn = sem("norm_chain", C), sem("deviation_ready", C), sem("x_normed2", C)
            c_xh = sem("xT_high2", C)
            c_r, c_ex, c_rw = sem("router_chain", C), sem("router_exp", C), sem("router_weights_split", C)

            def block_and_expert(t, e):
                return (t + 1, 0) if e == X else (t, e)

            def unit(t, l, e, o):
                return 2 * KH * (X * t + e) + KH * l + o

            def is_head(t):
                return isinstance(t, int) and t == 0

            def tiles(t):
                return 1 if is_head(t) else QT

            def rows(t):
                return HEAD if is_head(t) else P

            def width(t):
                return HEAD if is_head(t) else BT

            def first(t):
                return 0 if is_head(t) else HEAD + BT * (t - 1)

            def y_before(t):
                return 0 if is_head(t) else 9 * QT * t + 9 * (1 - QT)

            def m_before(t):
                return 2 if is_head(t) else 10 * t

            def xT_before(t):
                return 1 + QT * t

            def chain_before(t):
                return 0 if is_head(t) else 4 + (3 * QT + 1) * (t - 1)

            def schedule(t, ng, ahead):
                s, k, left = [], tiles(t), list(range(ng))
                at = {}

                def put(*step):
                    s.append(step)
                    for more in at.pop(step, ()):
                        put(*more)

                def group():
                    if left:
                        put("sum", left.pop(0))

                at["mid", 0, KH - 1] = [("weights",)]
                at["down", 0, k - 1] = [("turn", 0)]
                if k == QT:
                    at["mid", 1, KH - 1] = [("turn", 1)]
                    at["down", 1, k - 1] = [("turn", 2)]
                if ahead:
                    at["up", READ + 1, KH - 1] = [("read",)]
                    at["mid", READ + 1, 0] = [("residual", 1)]
                    at["mid", READ + 1, 1] = [("residual", 2)]
                    at["up", READ + 2, KH - 1] = [("scale",)]
                    at["down", READ + 1, k - 1] = [("xT", 0)]
                    at["mid", X - 1, 0] = [("xT", 1)]
                    at["mid", X - 1, 1] = [("xT", 2)]
                put("route",)
                group()
                for e in range(X):
                    for o in range(KH):
                        put("mid", e, o)
                    group()
                    if e + 1 < X:
                        for o in range(KH):
                            put("up", e + 1, o)
                        put("down", e, 0)
                    else:
                        put("down", e, 0)
                        if ahead:
                            for o in range(KH):
                                put("up", X, o)
                    for q in range(1, k):
                        put("down", e, q)
                    if e == BIAS - 1:
                        for q in range(k):
                            put("bias", q)
                    group()
                    if e == READ and ahead:
                        put("residual", 0)
                while left:
                    group()
                assert not at
                return s

            def vector_order(s):
                s = list(s)
                for n in range(len(s) - 1, -1, -1):
                    if s[n][0] == "up" and s[n][2] == KH - 1:
                        m = next((i for i in range(n, len(s)) if s[i][0] == "down"), n)
                        s.insert(m, s.pop(n))
                return s

            def out_slot(e):
                return BIAS if e is None else e + (e >= BIAS)

            PT = GT * PRO

            def slot_pro(i):
                return (i + SLOTS - PT % SLOTS) % SLOTS

            pro_uses = [sum(slot_pro(i) == s for i in range(PT)) for s in range(SLOTS)]
            blk_uses = [sum(i % SLOTS == s for i in range(GT * GB)) for s in range(SLOTS)]

            def group_slots(t, j):
                if t is None:
                    got = [(slot_pro(i), sum(slot_pro(k) == slot_pro(i) for k in range(i + 1)))
                           for i in range(GT * j, GT * (j + 1))]
                else:
                    got = [(i % SLOTS, pro_uses[i % SLOTS] + blk_uses[i % SLOTS] * t + i // SLOTS + 1)
                           for i in range(GT * j, GT * (j + 1))]
                return got, j % SS

            def group_number(t, j):
                return j if t is None else PRO + GB * t + j

            def after(t, j, k):
                n = group_number(t, j) + k if not isinstance(t, (int, type(None))) else None
                if n is not None:
                    return (t, j + k) if j + k < GB else (t + 1, j + k - GB)
                n = group_number(t, j) + k
                if n >= NG:
                    return None
                return (None, n) if n < PRO else ((n - PRO) // GB, (n - PRO) % GB)

            def program(step, blocks_loop):
                step(0, groups_of(0), True)
                blocks_loop(1, LAST - 1)
                step(LAST - 1, groups_of(LAST - 1), True)
                step(LAST, groups_of(LAST), False)

            def run(eng, step):
                def loop(a, b):
                    with eng.Fori(a, b) as t:
                        step(t, GB, True)
                program(step, loop)

            with nc.Block() as block:
                @block.sync
                def _(sp):
                    sp.dma_start(x1[0:HEAD, 0, :], x[0:HEAD, :]).then_inc(c_x, 16)

                    def step(t, ng, ahead):
                        if ahead:
                            sp.wait_ge(c_yd, y_before(t) + tiles(t))
                            sp.dma_start(x1[:, :, :], x[ds(first(t + 1), BT), :].rearrange("(q p) c -> p q c", p=P))\
                              .then_inc(c_x, 16)
                        sp.wait_ge(c_yd, y_before(t) + 9 * tiles(t))
                        if is_head(t):
                            sp.dma_start(out[0:HEAD, :], acc[0:HEAD, 0, :]).then_inc(c_out, 16)
                        else:
                            sp.dma_start(out[ds(first(t), BT), :].rearrange("(q p) c -> p q c", p=P), acc[:, :, :])\
                              .then_inc(c_out, 16)

                    run(sp, step)
                    sp.wait_ge(c_out, 16 * (LAST + 1))

                @block.gpsimd
                def _(pool):
                    def gather(t, j, ap):
                        got, _ = group_slots(t, j)
                        if not (t is None and j < 4):
                            pool.wait_ge(c_sum, group_number(t, j) - 3)
                            pool.sem_inc(c_freed, 1)
                        for i, (slot, _) in enumerate(got):
                            pool.indirect_dma_start(out=gat[:, slot, :], out_offset=None, in_=table,
                                                    in_offset=bass.IndirectOffsetOnAxis(ap=ap[:, i:i + 1], axis=0))\
                                .then_inc(c_gat[slot], 16)

                    for j in range(PRO):
                        gather(None, j, idx[:, GT * j:GT * (j + 1)])

                    def step(t, ng, ahead):
                        for k, (stage_t, lo, hi) in enumerate(((rowsA, 0, HG), (rowsB, HG, GB))):
                            if lo >= ng:
                                continue
                            n = min(hi, ng) - lo
                            if not is_head(t):
                                pool.wait_ge(c_sum, group_number(t, hi - GB))
                            nc.gpsimd.tensor_copy(stage_t[:, 0:GT * n], idx[:, ds(GT * group_number(t, lo), GT * n)])\
                                .then_inc(c_rows, 1)
                            pool.wait_ge(c_rows, 2 * t + k + 1)
                            for j in range(lo, lo + n):
                                gather(t, j, stage_t[:, GT * (j - lo):GT * (j - lo + 1)])

                    run(pool, step)

                @block.scalar
                def _(act):
                    def read_block(t):
                        nxt = 0 if t is None else t + 1
                        act.wait_ge(c_added, LEAD if t is None else PRO + GB * t + min(JP, GB if not isinstance(t, int) else groups_of(t)))
                        nc.scalar.activation(aggT[:, :, 0:width(nxt)], sumT[:, :, ds(first(nxt), width(nxt))], ACT.Relu)\
                            .then_inc(c_agg, 1)

                    def scale(t):
                        nxt = 0 if t is None else t + 1
                        r, q = rows(nxt), tiles(nxt)
                        act.wait_ge(c_st, chain_before(nxt) + 3 * q)
                        nc.scalar.activation(dev[0:r, 0:q, :], bmv[0:r, 0:q, 1:2], ACT.Sqrt, bias=eps[0:r, 0:1])\
                            .then_inc(c_dev, 1)

                    def xT(t, q):
                        nxt = 0 if t is None else t + 1
                        r = rows(nxt)
                        m = 1 if t is None else m_before(t) + 4 + tiles(t) + q
                        act.wait_ge(c_m, m + 1)
                        nc.scalar.copy(xh[:, :, q * P:q * P + r], psM[:, 0:2 * P].rearrange("p (h c) -> p h c", h=KH)[:, :, 0:r])\
                            .then_inc(c_xh, 1)

                    def layer(t, l, e, o):
                        t, e = block_and_expert(t, e)
                        w, u = width(t), unit(t, l, e, o)
                        hi, ps = (h1h, h2h)[l], psH[2 * l + o]
                        scale_ap, shift_ap = (bnp[:, 2 * l + k, KH * e + o:KH * e + o + 1] for k in range(2))
                        act.wait_ge(c_mm, u + 1)
                        nc.scalar.activation(hi[:, o, 0:w], ps[:, 0:w], ACT.Relu, bias=shift_ap, scale=scale_ap)
                        if not (is_head(t) and e == 0 and l == 0):
                            act.wait_ge(c_lo, u - 1)
                        nc.scalar.activation(act32[:, o, 0:w], ps[:, 0:w], ACT.Relu, bias=shift_ap, scale=scale_ap)\
                            .then_inc(c_act, 1)

                    read_block(None)
                    scale(None)
                    xT(None, 0)
                    for o in range(KH):
                        layer(0, 0, 0, o)

                    def step(t, ng, ahead):
                        for kind, *n in schedule(t, ng, ahead):
                            if kind == "up":
                                layer(t, 0, *n)
                            elif kind == "mid":
                                layer(t, 1, *n)
                            elif kind == "route":
                                act.wait_ge(c_r, 3 * t + 2)
                                r = rows(t)
                                nc.scalar.activation(ex[0:r, 0:tiles(t), :], lgm[0:r, 0:tiles(t), :], ACT.Exp).then_inc(c_ex, 1)
                            elif kind == "turn":
                                act.wait_ge(c_m, m_before(t) + 2 + n[0])
                                nc.scalar.copy(rwT[:, n[0], 0:rows(t)], psM[0:3 * X, 0:rows(t)]).then_inc(c_mr, 1)
                            elif kind == "read":
                                read_block(t)
                            elif kind == "scale":
                                scale(t)
                            elif kind == "xT":
                                xT(t, *n)

                    run(act, step)

                @block.vector
                def _(dve):
                    regs = [dve.alloc_register(f"window{j}") for j in range(GB)]

                    def select(t, j):
                        g = group_number(t, j)
                        slot = group_slots(t, j)[1]
                        if not (t is None and j < SS):
                            dve.wait_ge(c_sum, g - 4)
                        for i in range(GT):
                            col = GT * g + i
                            last = dve.scalar_tensor_tensor(
                                sel[:, slot, i, :, :], iota2[:, :, :], rel[:, ds(col, 1)],
                                wp[:, ds(col, 1), :].rearrange("p a c -> p (a c)").unsqueeze(2).to_broadcast([P, 2, W]),
                                ALU.is_equal, ALU.mult)
                        last.then_inc(c_sel, 1)

                    def add(t, j):
                        g = group_number(t, j)
                        at = dve.snap(regs[j], min_val=0, max_val=N - 1)
                        dve.wait_ge(c_sum, g + 1)
                        if not (t is None and j == 0):
                            dve.wait_ge(c_added, g)
                        dve.tensor_tensor(sumT[:, :, ds(at, W)], sumT[:, :, ds(at, W)], psA[:, :, 0, :], ALU.add)\
                           .then_inc(c_add1, 1)
                        dve.wait_ge(c_add1, g + 1)
                        dve.tensor_tensor(sumT[:, :, ds(at, W)], sumT[:, :, ds(at, W)], psA[:, :, 1, :], ALU.add)\
                           .then_inc(c_added, 1)

                    def sum_group(t, j):
                        nxt = after(t, j, 2)
                        if nxt is not None:
                            select(*nxt)
                        add(t, j)

                    def residual(t, q):
                        nxt = 0 if t is None else t + 1
                        r = rows(nxt)
                        m = 0 if t is None else m_before(t) + 1 + tiles(t) + q
                        dve.wait_ge(c_x, 16 * (nxt + 1))
                        dve.wait_ge(c_m, m + 1)
                        dve.tensor_tensor(x1[0:r, q, :], x1[0:r, q, :], psM[0:r, 0:D], ALU.add).then_inc(c_mr, 1)
                        dve.wait_ge(c_mr, m + 1)
                        c = chain_before(nxt) + 3 * q
                        dve.bn_stats(bst[0:r, q, :], x1[0:r, q, :]).then_inc(c_st, 1)
                        dve.wait_ge(c_st, c + 1)
                        dve.sem_inc(c_st, 1)
                        dve.bn_aggr(bmv[0:r, q, :], bst[0:r, q, :]).then_inc(c_st, 1)

                    def scale(t):
                        nxt = 0 if t is None else t + 1
                        r, k = rows(nxt), tiles(nxt)
                        dve.wait_ge(c_dev, nxt + 1)
                        dve.reciprocal(inv[0:r, 0:k, :], dev[0:r, 0:k, :]).then_inc(c_st, 1)
                        dve.wait_ge(c_st, chain_before(nxt) + 3 * k + 1)
                        for q in range(k):
                            dve.tensor_scalar(xn2[0:r, q, :], x1[0:r, q, :], bmv[0:r, q, 0:1], inv[0:r, q, :],
                                              ALU.subtract, ALU.mult).then_inc(c_xn, 1)

                    def xT(t, q):
                        nxt = 0 if t is None else t + 1
                        r = rows(nxt)
                        dve.wait_ge(c_xh, 1 if t is None else xT_before(t) + q + 1)
                        dve.tensor_tensor(xl[:, :, q * P:q * P + r],
                                          psM[:, 0:2 * P].rearrange("p (h c) -> p h c", h=KH)[:, :, 0:r],
                                          xh[:, :, q * P:q * P + r], ALU.subtract).then_inc(c_mr, 1)

                    def route(t):
                        r, k = rows(t), tiles(t)
                        dve.wait_ge(c_m, m_before(t) + 1)
                        dve.tensor_tensor(lg[0:r, 0:k, :], psM[0:r, 0:k * X].rearrange("p (q e) -> p q e", e=X),
                                          brb[0:r, :].unsqueeze(1).to_broadcast([r, k, X]), ALU.add).then_inc(c_mr, 1)
                        dve.wait_ge(c_mr, m_before(t) + 1)
                        dve.tensor_reduce(mx[0:r, 0:k], lg[0:r, 0:k, :], AX.X, ALU.max).then_inc(c_r, 1)
                        dve.wait_ge(c_r, 3 * t + 1)
                        dve.tensor_tensor(lgm[0:r, 0:k, :], lg[0:r, 0:k, :], mx[0:r, 0:k].unsqueeze(2).to_broadcast([r, k, X]),
                                          ALU.subtract).then_inc(c_r, 1)

                    def weights(t):
                        r, k = rows(t), tiles(t)
                        dve.wait_ge(c_ex, t + 1)
                        dve.tensor_reduce(sm[0:r, 0:k], ex[0:r, 0:k, :], AX.X, ALU.add).then_inc(c_r, 1)
                        dve.wait_ge(c_r, 3 * t + 3)
                        dve.reciprocal(mx[0:r, 0:k], sm[0:r, 0:k]).then_inc(c_rw, 1)
                        dve.wait_ge(c_rw, 4 * t + 1)
                        dve.tensor_tensor(rw[0:r, 0:k, :], ex[0:r, 0:k, :], mx[0:r, 0:k].unsqueeze(2).to_broadcast([r, k, X]),
                                          ALU.mult).then_inc(c_rw, 1)
                        dve.wait_ge(c_rw, 4 * t + 2)
                        dve.tensor_copy(rw24[0:r, 0:k, 0:X], rw[0:r, 0:k, :])
                        dve.tensor_copy(rw24[0:r, 0:k, 2 * X:3 * X], rw[0:r, 0:k, :]).then_inc(c_rw, 1)
                        dve.wait_ge(c_rw, 4 * t + 3)
                        dve.tensor_tensor(rw24[0:r, 0:k, X:2 * X], rw[0:r, 0:k, :], rw24[0:r, 0:k, 0:X], ALU.subtract)\
                           .then_inc(c_rw, 1)

                    def layer(t, l, e, o):
                        t, e = block_and_expert(t, e)
                        w, u = width(t), unit(t, l, e, o)
                        hi, lo = ((h1h, h1l), (h2h, h2l))[l]
                        dve.wait_ge(c_act, u + 1)
                        dve.tensor_tensor(lo[:, o, 0:w], act32[:, o, 0:w], hi[:, o, 0:w], ALU.subtract).then_inc(c_lo, 1)

                    def down(t, e, q):
                        r, v = rows(t), out_slot(e) * tiles(t) + q
                        dve.wait_ge(c_y, y_before(t) + v + 1)
                        if e == 0 and q == 0 and not is_head(t):
                            dve.wait_ge(c_out, 16 * t)
                        if e != 0:
                            dve.wait_ge(c_yd, y_before(t) + v - tiles(t) + 1)
                        if e is None:
                            dve.tensor_tensor(acc[0:r, q, :], acc[0:r, q, :], psY[v % 2][0:r, :], ALU.add)\
                               .then_inc(c_yd, 1)
                        else:
                            dve.scalar_tensor_tensor(acc[0:r, q, :], psY[v % 2][0:r, :], rw[0:r, q, e:e + 1],
                                                     (acc if e else x1)[0:r, q, :], ALU.mult, ALU.add).then_inc(c_yd, 1)

                    dve.load(regs[0:PRO], base[0:1, 0:PRO])
                    select(None, 0)
                    select(None, 1)
                    for j in range(LEAD):
                        sum_group(None, j)
                    residual(None, 0)
                    scale(None)
                    xT(None, 0)
                    layer(0, 0, 0, 0)
                    layer(0, 0, 0, 1)
                    for j in range(LEAD, PRO):
                        sum_group(None, j)

                    def step(t, ng, ahead):
                        if ng:
                            dve.load(regs[0:ng], base[0:1, ds(PRO + GB * t, ng)])
                        for kind, *n in vector_order(schedule(t, ng, ahead)):
                            if kind == "sum":
                                sum_group(t, *n)
                            elif kind == "route":
                                route(t)
                            elif kind == "weights":
                                weights(t)
                            elif kind == "up":
                                layer(t, 0, *n)
                            elif kind == "mid":
                                layer(t, 1, *n)
                            elif kind == "down":
                                down(t, *n)
                            elif kind == "bias":
                                down(t, None, *n)
                            elif kind == "residual":
                                residual(t, *n)
                            elif kind == "scale":
                                scale(t)
                            elif kind == "xT":
                                xT(t, *n)

                    run(dve, step)

                @block.tensor
                def _(pe):
                    def sum_group(t, j):
                        got, s = group_slots(t, j)
                        g = group_number(t, j)
                        pe.wait_ge(c_sel, g + 1)
                        if not (t is None and j == 0):
                            pe.wait_ge(c_added, g)
                        for slot, count in got:
                            pe.wait_ge(c_gat[slot], 16 * count)
                        for h in range(KH):
                            for i, (slot, _) in enumerate(got):
                                nc.tensor.matmul(psA[:, h, :, :], gat[:, slot, h * P:(h + 1) * P], sel[:, s, i, :, :],
                                                 start=(i == 0), stop=False)
                                last = nc.tensor.matmul(psA[:, h, 0, :], gat[:, slot, D + h * P:D + (h + 1) * P],
                                                        sel[:, s, i, 0, :], start=False, stop=(i == GT - 1))
                        last.then_inc(c_sum, 1)

                    def misc_free(m):
                        if not (isinstance(m, int) and m == 0):
                            pe.wait_ge(c_mr, m)

                    def residual(t, q):
                        nxt = 0 if t is None else t + 1
                        r = rows(nxt)
                        m = 0 if t is None else m_before(t) + 1 + tiles(t) + q
                        pe.wait_ge(c_agg, nxt + 1)
                        misc_free(m)
                        for h in range(KH):
                            last = nc.tensor.transpose(psM[0:r, h * P:(h + 1) * P], aggT[:, h, q * P:q * P + r], ident[:, :])
                        last.then_inc(c_m, 1)

                    def xT(t, q):
                        nxt = 0 if t is None else t + 1
                        r = rows(nxt)
                        m = 1 if t is None else m_before(t) + 4 + tiles(t) + q
                        pe.wait_ge(c_xn, 1 if t is None else xT_before(t) + q + 1)
                        misc_free(m)
                        for h in range(KH):
                            last = nc.tensor.transpose(psM[:, h * P:h * P + r], xn2[0:r, q, h * P:(h + 1) * P],
                                                       ident[0:r, 0:r])
                        last.then_inc(c_m, 1)

                    def route(t):
                        r, k = rows(t), tiles(t)
                        misc_free(m_before(t))
                        for q in range(k):
                            n = 0
                            for h in range(KH):
                                for a, b in ((xh, Wrh), (xh, Wrl), (xl, Wrh)):
                                    last = nc.tensor.matmul(psM[0:r, q * X:(q + 1) * X], a[:, h, q * P:q * P + r], b[:, h, :],
                                                            start=(n == 0), stop=(n == 5))
                                    n += 1
                        last.then_inc(c_m, 1)

                    def turn(t, q):
                        r = rows(t)
                        if q == 0:
                            pe.wait_ge(c_rw, 4 * t + 4)
                        misc_free(m_before(t) + 1 + q)
                        nc.tensor.transpose(psM[0:3 * X, 0:r], rw24[0:r, q, :].bitcast(f32), ident[0:r, 0:r])\
                          .then_inc(c_m, 1)

                    def layer(t, l, e, o):
                        t, e = block_and_expert(t, e)
                        w, u = width(t), unit(t, l, e, o)
                        wh, wl = ((W1h, W1l), (W2h, W2l))[l]
                        hi, lo = ((xh, xl), (h1h, h1l))[l]
                        if o == 0:
                            if l == 1:
                                pe.wait_ge(c_lo, unit(t, 0, e, KH))
                            else:
                                pe.wait_ge(c_mr, m_before(t))
                        if not (is_head(t) and e == 0):
                            pe.wait_ge(c_act, u - 3)
                        n = 0
                        for h in range(KH):
                            for a, b in ((wh, hi), (wh, lo), (wl, hi)):
                                last = nc.tensor.matmul(psH[2 * l + o][:, 0:w], a[:, e, h, o * P:(o + 1) * P],
                                                        b[:, h, 0:w], start=(n == 0), stop=(n == 5))
                                n += 1
                        last.then_inc(c_mm, 1)

                    def out_free(t, v):
                        if not (is_head(t) and v < 2):
                            pe.wait_ge(c_yd, y_before(t) + max(v - 1, 0))

                    def down(t, e, q):
                        r, v = rows(t), out_slot(e) * tiles(t) + q
                        if q == 0:
                            pe.wait_ge(c_lo, unit(t, 1, e, KH))
                        out_free(t, v)
                        n = 0
                        for h in range(KH):
                            for a, b in ((h2h, Woh), (h2h, Wol), (h2l, Woh)):
                                last = nc.tensor.matmul(psY[v % 2][0:r, :], a[:, h, q * P:q * P + r], b[:, e, h, :],
                                                        start=(n == 0), stop=(n == 5))
                                n += 1
                        last.then_inc(c_y, 1)

                    def bias(t, q):
                        r, v = rows(t), out_slot(None) * tiles(t) + q
                        if q == 0:
                            pe.wait_ge(c_mr, m_before(t) + 1 + tiles(t))
                        out_free(t, v)
                        nc.tensor.matmul(psY[v % 2][0:r, :], rwT[:, q, 0:r], bo24[:, :], start=True, stop=True)\
                          .then_inc(c_y, 1)

                    for j in range(LEAD):
                        sum_group(None, j)
                    residual(None, 0)
                    xT(None, 0)
                    layer(0, 0, 0, 0)
                    layer(0, 0, 0, 1)
                    for j in range(LEAD, PRO):
                        sum_group(None, j)

                    def step(t, ng, ahead):
                        for kind, *n in schedule(t, ng, ahead):
                            if kind == "sum":
                                sum_group(t, *n)
                            elif kind == "route":
                                route(t)
                            elif kind == "turn":
                                turn(t, *n)
                            elif kind == "up":
                                layer(t, 0, *n)
                            elif kind == "mid":
                                layer(t, 1, *n)
                            elif kind == "down":
                                down(t, *n)
                            elif kind == "bias":
                                bias(t, *n)
                            elif kind == "residual":
                                residual(t, *n)
                            elif kind == "xT":
                                xT(t, *n)

                    run(pe, step)


_INS = ["x", "src", "dst", "edge_type_8", "edge_weight", "L0_gnn_weight", "L0_ffn_Wr", "L0_ffn_br",
        "L0_ffn_W1", "L0_ffn_b1", "L0_ffn_g1", "L0_ffn_be1", "L0_ffn_m1", "L0_ffn_v1",
        "L0_ffn_W2", "L0_ffn_b2", "L0_ffn_g2", "L0_ffn_be2", "L0_ffn_m2", "L0_ffn_v2", "L0_ffn_Wo", "L0_ffn_bo"]


def kernel(**inputs):
    import numpy as np
    import concourse.bacc as bacc
    from concourse import mybir as mb
    from concourse.bass_utils import run_bass_kernel_spmd

    nc = bacc.Bacc("TRN2", target_bir_lowering=False, num_devices=1)
    arrays, args = {}, []
    for name in _INS:
        a = np.ascontiguousarray(inputs[name])
        arrays[f"in_{name}"] = a
        args.append(nc.dram_tensor(f"in_{name}", a.shape, mb.dt.from_np(a.dtype), kind="ExternalInput").ap())
    low = lower_bounds()
    arrays["in_low"] = low
    args.append(nc.dram_tensor("in_low", low.shape, mb.dt.float32, kind="ExternalInput").ap())
    args.append(nc.dram_tensor("out", (N, D), mb.dt.float32, kind="ExternalOutput").ap())
    gnn_ffn(nc, *args)
    r = run_bass_kernel_spmd(nc, [arrays], core_ids=[0])
    return r.results[0]["out"]
```

```python
import concourse.bass as bass
from concourse import mybir
from contextlib import ExitStack

N = 6250
D = 256
E = 106250
R = 8
X = 8
KH = D // 128
P = 128
BN_EPS = 0.001
LN_EPS = 1e-5

GT = 3
GE = GT * P
NG = -(-E // GE)
W = 32
CH = 3
CG = -(-NG // CH)
COLS = CH * CG * GT

QT = 3
BT = QT * P
HEAD = N % BT
HIDDEN = 256
NBLK = N // BT
GB = 17
LEAD = 7
PRO = 12
JP = LEAD + GB - PRO
READ = 5
HB = 3
BIAS = 4
LAST = NBLK
WS = 250
NW = -(-N // WS)
NP = NW * WS + W

EARLY = 2
SLOTS = 17
SS = 6


def groups_of(t):
    return max(0, min(GB, NG - PRO - GB * t))


def lower_bounds():
    import numpy as np
    g = np.arange(CH * CG)
    low = np.where(g >= LEAD, HEAD + BT * ((g - LEAD) // GB), 0)
    low = np.where(g < NG, np.minimum(low, N), 0)
    return np.ascontiguousarray(low.reshape(CH, CG).T.astype(np.float32))


def gnn_ffn(nc, x, src, dst, etype, weight_e, wg, wr, br, w1, b1, g1, be1, m1, v1,
            w2, b2, g2, be2, m2, v2, wo, bo, low, out):
    dt = mybir.dt
    f32, f32r, f16, i32 = dt.float32, dt.float32r, dt.float16, dt.int32
    ALU, ACT, AX = mybir.AluOpType, mybir.ActivationFunctionType, mybir.AxisListType
    ds = bass.ds

    table = nc.dram_tensor("messages_table", [N * R, 2 * D], f16).ap()

    rows_of = nc.dram_tensor("edge_rows", [P, COLS], i32).ap()
    nodes = nc.dram_tensor("edge_nodes", [P, COLS], f32).ap()

    keep = ExitStack()
    with keep:
        def sb(name, shape, d, ctx=keep):
            return ctx.enter_context(nc.sbuf_tensor(name, shape, d))

        def sem(name, ctx=keep):
            return ctx.enter_context(nc.semaphore(name))

        W1h, W1l = sb("W1h", [P, X, KH, D], f32r), sb("W1l", [P, X, KH, D], f32r)
        W2h, W2l = sb("W2h", [P, X, KH, D], f32r), sb("W2l", [P, X, KH, D], f32r)
        Woh, Wol = sb("Woh", [P, X, KH, D], f32r), sb("Wol", [P, X, KH, D], f32r)
        Wr2 = sb("Wr2", [P, KH, 2, X], f32r)
        bo24 = sb("bo24", [3 * X, D], f32r)
        brb = sb("brb", [P, X], f32)
        ident = sb("ident", [P, P], f32)
        iota2 = sb("iota2", [P, 2, W], f16)
        eps = sb("eps", [P, 1], f32)
        bnp = sb("bnp", [P, 4, 2 * X], f32)
        rel = sb("rel", [P, COLS], f32)
        wp = sb("wp", [P, COLS, 2], f16)
        base = sb("base", [1, CH * CG], i32)
        bad = sb("bad", [1, 1], i32)

        s_table = sem("table_stored")

        A = ExitStack()
        with A:
            idx = sb("idx", [P, COLS], i32, A)
            node = sb("node", [P, COLS], f32, A)
            Wgh, Wgl = sb("Wgh", [P, KH, R, D], f32r, A), sb("Wgl", [P, KH, R, D], f32r, A)
            fraw = sb("fraw", [P, 2, KH, D], f32, A)
            xin = sb("xin", [P, 2, D], f32, A)
            xn = sb("xn", [P, 2, D], f32, A)
            xTh, xTl = sb("xTh", [P, 2, KH, P], f32r, A), sb("xTl", [P, 2, KH, P], f32r, A)
            stage = sb("stage", [P, 2, R, 2 * D], f16, A)
            slots = stage[:, :, :, :].rearrange("p s r c -> p (s r c)").bitcast(f32)\
                .rearrange("p (s w k n) -> p s w k n", s=2, k=KH, n=D)
            wraw = [slots[:, 1 - r % 2, r // 2, :, :] for r in range(R)]
            st6, mv, sd = sb("st6", [P, 6], f32, A), sb("mv", [P, 2], f32, A), sb("sd", [P, 2], f32, A)
            e_src, e_dst = sb("e_src", [CG, CH, GE], i32, A), sb("e_dst", [CG, CH, GE], i32, A)
            e_typ, e_w = sb("e_typ", [CG, CH, GE], i32, A), sb("e_w", [CG, CH, GE], f32, A)
            e_row = e_src[:, :, :].bitcast(f32)
            e_node = sb("e_node", [CG, CH, GE], f32, A)
            e_rel = e_dst[:, :, :].bitcast(f32)
            gmin, gmax = sb("gmin", [CG, CH], f32, A), sb("gmax", [CG, CH], f32, A)
            lowt, viol = sb("lowt", [CG, CH], f32, A), sb("viol", [CG, 2, CH], f32, A)
            vio2 = sb("vio2", [CG, 2], f32, A)
            ones = sb("ones", [P, P], f32, A)
            praw = sb("praw", [2 * X, 10, P], f32, A)
            wrr = sb("wrr", [P, KH, X], f32, A)
            bor = sb("bor", [X, D], f32, A)
            boh, bol = sb("boh", [X, D], f32r, A), sb("bol", [X, D], f32r, A)
            psT = [A.enter_context(nc.psum_tensor(f"psT{i}", [P, KH, P], f32)) for i in range(1)]
            psP = [A.enter_context(nc.psum_tensor(f"psP{i}", [P, 2, D], f32)) for i in range(4)]
            psE = A.enter_context(nc.psum_tensor("psE", [P, 512], f32))

            s_eps, s_wpad = sem("eps_set", A), sem("weight_padding_zero", A)
            s_edge, s_par = sem("edges_loaded", A), sem("params_loaded", A)
            s_wgl = [sem(f"wg_loaded{i}", A) for i in range(R)]
            s_wgh, s_wgd = sem("wg_high", A), sem("wg_split", A)
            s_x = [sem(f"x_loaded{i}", A) for i in range(2)]
            s_ln, s_sd, s_xn = sem("ln_chain", A), sem("deviation", A), sem("x_normed", A)
            s_tr, s_xh, s_xl = sem("x_transposed", A), sem("xT_high", A), sem("xT_low", A)
            s_mm, s_th, s_tl = sem("messages_done", A), sem("table_high", A), sem("table_low", A)
            s_st = [sem(f"stage_stored{i}", A) for i in range(2)]
            s_nd = sem("nodes_stored", A)
            s_node, s_el = sem("edge_nodes", A), sem("edge_chain", A)
            s_p, s_ep = sem("pool_chain", A), sem("edges_prepared", A)
            s_bn, s_bs = sem("bn_chain", A), sem("bn_root", A)
            s_et, s_ee = sem("edge_transposed", A), sem("edge_evacuated", A)
            s_fl = [sem(f"ffn_loaded{i}", A) for i in range(2)]
            s_fd = sem("ffn_split", A)
            s_wh = sem("edge_weight_high", A)
            s_bo, s_bom = sem("bo_split", A), sem("bo_placed", A)

            NT = -(-N // P)
            TAIL = N - (NT - 1) * P
            PAIRS = R // 2
            FULL = NG - 1 - (CH - 1) * CG
            PADS = CG - FULL - 1
            NEDGE = 3 * (CH + 2 + PADS) + (CH + 1) + 1
            NPAR = 13
            ffn = [(hi, lo, a, e) for hi, lo, a in ((W1h, W1l, w1), (W2h, W2l, w2), (Woh, Wol, wo)) for e in range(X)]
            PREP = 4
            edge_jobs = [(q, c) for q in range(4) for c in range(CH)]
            NJ = len(edge_jobs)

            with nc.Block() as block:
                @block.sync
                def _(sp):
                    for s in range(2):
                        sp.dma_start(xin[:, s, :], x[s * P:(s + 1) * P, :]).then_inc(s_x[s], 16)
                    def load_x(t, s, rows):
                        sp.wait_ge(s_xn, t - 1)
                        sp.dma_start(xin[0:rows, s, :], x[N - rows:N, :] if rows < P else x[ds(t * P, P), :])\
                            .then_inc(s_x[s], 16)

                    load_x(2, 0, P)
                    o = (CH - 1) * CG * GE
                    left = E - o - FULL * GE
                    for tile, a in ((e_dst, dst), (e_src, src), (e_typ, etype), (e_w, weight_e)):
                        for c in range(CH - 1):
                            sp.dma_start(tile[:, c, :], a[c * CG * GE:(c + 1) * CG * GE]
                                         .rearrange("(g k) -> g k", k=GE)).then_inc(s_edge, 16)
                        if tile is e_w:
                            sp.wait_ge(s_wpad, 1)
                        sp.dma_start(tile[0:FULL, CH - 1, :], a[o:o + FULL * GE]
                                     .rearrange("(g k) -> g k", k=GE)).then_inc(s_edge, 16)
                        sp.dma_start(tile[FULL:FULL + 1, CH - 1, 0:left],
                                     a[E - left:E].rearrange("(g k) -> g k", k=left)).then_inc(s_edge, 16)
                        if tile is not e_w:
                            sp.dma_start(tile[FULL:FULL + 1, CH - 1, left:GE],
                                         a[E - GE + left:E].rearrange("(g k) -> g k", k=GE - left)).then_inc(s_edge, 16)
                            for g in range(FULL + 1, CG):
                                sp.dma_start(tile[g:g + 1, CH - 1, :],
                                             a[E - GE:E].rearrange("(g k) -> g k", k=GE)).then_inc(s_edge, 16)
                    sp.dma_start(lowt[:, :], low).then_inc(s_edge, 16)

                    def tile_io(t, s, more):
                        if more:
                            load_x(t + 3, 1 - s, more)
                        sp.wait_ge(s_tl, PAIRS * (t + 1))
                        sp.dma_start(table[ds(t * P * R, P * R), :].rearrange("(p r) c -> p (r c)", r=R),
                                     stage[:, s, :, :].rearrange("p r c -> p (r c)")).then_inc(s_st[s], 16)

                    with sp.Fori(0, NT // 2 - 2) as i:
                        for s in range(2):
                            tile_io(2 * i + s, s, P)
                    sp.wait_ge(s_bo, 2)
                    for k, part in enumerate((boh, boh, bol)):
                        sp.dma_start(bo24[k * X:(k + 1) * X, :].bitcast(f32), part[:, :].bitcast(f32)).then_inc(s_bom, 16)
                    sp.wait_ge(s_ee, NJ)
                    sp.dma_start(nodes, node[:, :]).then_inc(s_nd, 16)
                    sp.dma_start(rows_of, idx[:, :]).then_inc(s_nd, 16)
                    tile_io(NT - 5, 0, P)
                    tile_io(NT - 4, 1, TAIL)
                    tile_io(NT - 3, 0, 0)
                    tile_io(NT - 2, 1, 0)
                    for half in range(2):
                        sp.wait_ge(s_tl, PAIRS * (NT - 1) + (half + 1) * PAIRS // 2)
                        part = slice(half * R // 2, (half + 1) * R // 2)
                        sp.dma_start(table[(NT - 1) * P * R:N * R, :].rearrange("(p r) c -> p r c", r=R)[:, part, :],
                                     stage[0:TAIL, 0, part, :]).then_inc(s_st[0], 16)
                    sp.wait_ge(s_bom, 48)
                    sp.wait_ge(s_nd, 32)
                    sp.wait_ge(s_st[0], 16 * (NT // 2 + 2))
                    sp.wait_ge(s_st[1], 16 * (NT // 2))

                @block.scalar
                def _(act):
                    for r in range(R):
                        act.dma_start(wraw[r], wg[r, :, :].rearrange("(k p) n -> p k n", p=P))\
                           .then_inc(s_wgl[r], 16)
                    def load_params():
                        for a, j in ((g1, 0), (v1, 1), (b1, 2), (m1, 3), (be1, 4),
                                     (g2, 5), (v2, 6), (b2, 7), (m2, 8), (be2, 9)):
                            act.dma_start(praw[:, j, :], a.rearrange("e (h p) -> (e h) p", p=P)).then_inc(s_par, 16)
                        act.dma_start(wrr[:, :, :], wr.rearrange("(k p) n -> p k n", p=P)).then_inc(s_par, 16)
                        act.dma_start(bor[:, :], bo).then_inc(s_par, 16)
                        act.dma_start(brb[:, :], br.rearrange("(a n) -> a n", a=1).to_broadcast([P, X])).then_inc(s_par, 16)

                    def deviation(t):
                        act.wait_ge(s_ln, 4 * t + 3)
                        nc.scalar.activation(sd[:, 0:1], mv[:, 1:2], ACT.Sqrt, bias=eps[:, 0:1]).then_inc(s_sd, 1)

                    def xT_high(t, s, rows):
                        act.wait_ge(s_tr, t + 1)
                        nc.scalar.copy(xTh[:, s, :, 0:rows], psT[0][:, :, 0:rows]).then_inc(s_xh, 1)

                    def t_high(t, s, k, rows, stored):
                        act.wait_ge(s_mm, PAIRS * t + k + 1)
                        if k == 0 and stored is not None:
                            act.wait_ge(s_st[s], 16 * stored)
                        nc.scalar.copy(stage[0:rows, s, 2 * k:2 * k + 2, 0:D], psP[k][0:rows, :, :]).then_inc(s_th, 1)

                    def evacuate(n):
                        act.wait_ge(s_et, n + 1)
                        if n < NJ:
                            q, c = edge_jobs[n]
                            lot = (idx[:, :], rel[:, :], wp[:, :, 0], node[:, :])[q]
                            nc.scalar.copy(lot[:, GT * CG * c:GT * CG * (c + 1)].rearrange("p (g i) -> p i g", i=GT),
                                           psE[:, 0:GT * CG].rearrange("p (i g) -> p i g", i=GT))\
                                .then_inc(s_wh if q == 2 else s_ee, 1)
                        elif n == NJ:
                            nc.scalar.copy(base[0:1, :], psE[0:1, 0:CH * CG]).then_inc(s_ee, 1)
                        else:
                            nc.scalar.copy(bnp[:, :, :], psE[:, 0:8 * X].rearrange("p (q c) -> p q c", q=4)).then_inc(s_ee, 1)

                    def tile(t, s, rows_next, stored, ahead=True, jobs=None):
                        for k in range(PAIRS):
                            t_high(t, s, k, P, stored)
                            if k == 1:
                                xT_high(t + 1, 1 - s, rows_next)
                            if jobs is not None and PAIRS * jobs + k < NJ + 2:
                                evacuate(PAIRS * jobs + k)
                            if k == 2 and ahead:
                                deviation(t + 2)

                    deviation(0)
                    for r in range(R):
                        act.wait_ge(s_wgl[r], 16)
                        nc.scalar.copy(Wgh[:, :, r, :], wraw[r]).then_inc(s_wgh, 1)
                        if r == 0:
                            xT_high(0, 0, P)
                            deviation(1)
                    load_params()
                    tile(0, 0, P, None)
                    tile(1, 1, P, None)
                    with act.Fori(1, EARLY) as i:
                        for s in range(2):
                            tile(2 * i + s, s, P, i)
                    for t in range(2 * EARLY, 2 * EARLY + PREP):
                        tile(t, t % 2, P, t // 2)
                        if t == 2 * EARLY + 2:
                            act.wait_ge(s_bn, 2)
                            nc.scalar.activation(praw[:, 1, :], praw[:, 1, :], ACT.Sqrt)
                            nc.scalar.activation(praw[:, 6, :], praw[:, 6, :], ACT.Sqrt).then_inc(s_bs, 1)
                    for t in range(2 * EARLY + PREP, 2 * EARLY + 2 * PREP):
                        tile(t, t % 2, P, t // 2, jobs=t - 2 * EARLY - PREP)
                    with act.Fori(EARLY + PREP, NT // 2 - 1) as i:
                        for s in range(2):
                            tile(2 * i + s, s, P, i)
                    tile(NT - 3, 0, P, NT // 2 - 1)
                    tile(NT - 2, 1, TAIL, NT // 2 - 1, ahead=False)
                    for k in range(PAIRS):
                        t_high(NT - 1, 0, k, TAIL, NT // 2)

                @block.vector
                def _(dve):
                    dve.memset(eps[:, :], LN_EPS).then_inc(s_eps, 1)

                    def stats(t, s, c, rows):
                        dve.wait_ge(s_x[s], 16 * (c + 1))
                        dve.bn_stats(st6[0:rows, :], xin[0:rows, s, :]).then_inc(s_ln, 1)
                        dve.wait_ge(s_ln, 4 * t + 1)
                        dve.sem_inc(s_ln, 1)
                        dve.bn_aggr(mv[0:rows, :], st6[0:rows, :]).then_inc(s_ln, 1)

                    def norm(t, s, rows):
                        dve.wait_ge(s_sd, t + 1)
                        dve.reciprocal(sd[0:rows, 1:2], sd[0:rows, 0:1]).then_inc(s_ln, 1)
                        dve.wait_ge(s_ln, 4 * t + 4)
                        dve.tensor_scalar(xn[0:rows, s, :], xin[0:rows, s, :], mv[0:rows, 0:1], sd[0:rows, 1:2],
                                          ALU.subtract, ALU.mult).then_inc(s_xn, 1)

                    def xT_low(t, s, rows):
                        dve.wait_ge(s_xh, t + 1)
                        dve.tensor_tensor(xTl[:, s, :, 0:rows], psT[0][:, :, 0:rows], xTh[:, s, :, 0:rows],
                                          ALU.subtract).then_inc(s_xl, 1)

                    def t_low(t, s, k, rows):
                        dve.wait_ge(s_th, PAIRS * t + k + 1)
                        dve.tensor_tensor(stage[0:rows, s, 2 * k:2 * k + 2, D:2 * D], psP[k][0:rows, :, :],
                                          stage[0:rows, s, 2 * k:2 * k + 2, 0:D], ALU.subtract).then_inc(s_tl, 1)

                    def weights_low(c):
                        dve.wait_ge(s_wh, c + 1)
                        part = slice(GT * CG * c, GT * CG * (c + 1))
                        dve.tensor_tensor(wp[:, part, 1].rearrange("p (g i) -> p i g", i=GT),
                                          psE[:, 0:GT * CG].rearrange("p (i g) -> p i g", i=GT),
                                          wp[:, part, 0].rearrange("p (g i) -> p i g", i=GT), ALU.subtract)\
                           .then_inc(s_ee, 1)

                    def tile(t, s, c, rows_next, rows_behind=P, jobs=None):
                        for k in range(PAIRS):
                            t_low(t, s, k, P)
                            if k == 1:
                                xT_low(t + 1, 1 - s, rows_next)
                                if rows_behind:
                                    stats(t + 2, s, c, rows_behind)
                            if k == 3 and rows_behind:
                                norm(t + 2, s, rows_behind)
                            if jobs is not None and PAIRS * jobs + k < NJ and edge_jobs[PAIRS * jobs + k][0] == 2:
                                weights_low(edge_jobs[PAIRS * jobs + k][1])

                    n = {s_el: 0, s_bn: 0}

                    def link(ins, chain):
                        n[chain] += 1
                        ins.then_inc(chain, 1)
                        dve.wait_ge(chain, n[chain])

                    def edges_least_greatest():
                        dve.wait_ge(s_node, 1)
                        link(dve.tensor_reduce(gmax[:, :], e_node[:, :, :], AX.X, ALU.max), s_el)
                        link(dve.tensor_reduce(gmin[:, :], e_node[:, :, :], AX.X, ALU.min), s_el)

                    def edges_relative():
                        link(dve.tensor_tensor(viol[:, 0, :], gmax[:, :], gmin[:, :], ALU.subtract), s_el)
                        link(dve.tensor_scalar(viol[:, 0, :], viol[:, 0, :], W - 0.5, None, ALU.is_gt), s_el)
                        link(dve.tensor_tensor(viol[:, 1, :], gmin[:, :], lowt[:, :], ALU.is_lt), s_el)
                        link(dve.tensor_tensor(viol[:, 0, :], viol[:, 0, :], viol[:, 1, :], ALU.add), s_el)
                        link(dve.tensor_reduce(vio2[:, 0:1], viol[:, 0, :], AX.X, ALU.add), s_el)
                        link(dve.tensor_copy(vio2[:, 1:2], vio2[:, 0:1]), s_el)
                        for c in range(CH):
                            last = dve.tensor_scalar(e_rel[:, c, :], e_node[:, c, :], gmin[:, c:c + 1], None,
                                                     ALU.subtract)
                        last.then_inc(s_ep, 1)

                    def add_eps():
                        dve.wait_ge(s_par, 16 * NPAR)
                        link(dve.tensor_scalar(praw[:, 1, :], praw[:, 1, :], BN_EPS, None, ALU.add), s_bn)
                        link(dve.tensor_scalar(praw[:, 6, :], praw[:, 6, :], BN_EPS, None, ALU.add), s_bn)

                    def fold_batch_norm(l):
                        g, v, b, m, be = (praw[:, 5 * l + k, :] for k in range(5))
                        dve.wait_ge(s_bs, 1)
                        link(dve.reciprocal(v, v), s_bn)
                        link(dve.tensor_tensor(g, g, v, ALU.mult), s_bn)
                        link(dve.tensor_tensor(b, b, m, ALU.subtract), s_bn)
                        link(dve.tensor_tensor(b, b, g, ALU.mult), s_bn)
                        link(dve.tensor_tensor(b, b, be, ALU.add), s_bn)

                    dve.wait_ge(s_eps, 1)
                    dve.memset(mv[:, :], 0.0).then_inc(s_eps, 1)
                    dve.wait_ge(s_eps, 2)
                    stats(0, 0, 0, P)
                    norm(0, 0, P)
                    for r in range(R):
                        dve.wait_ge(s_wgh, r + 1)
                        dve.tensor_tensor(Wgl[:, :, r, :], wraw[r], Wgh[:, :, r, :], ALU.subtract)\
                           .then_inc(s_wgd, 1)
                        if r == 0:
                            xT_low(0, 0, P)
                            stats(1, 1, 0, P)
                            norm(1, 1, P)
                    tile(0, 0, 1, P)
                    tile(1, 1, 1, P)
                    with dve.Fori(1, EARLY) as i:
                        for s in range(2):
                            tile(2 * i + s, s, i + 1, P)
                    for t in range(2 * EARLY, 2 * EARLY + PREP):
                        tile(t, t % 2, t // 2 + 1, P)
                        if t == 2 * EARLY:
                            edges_least_greatest()
                        elif t == 2 * EARLY + 1:
                            edges_relative()
                            add_eps()
                        else:
                            fold_batch_norm(t - 2 * EARLY - 2)
                    for t in range(2 * EARLY + PREP, 2 * EARLY + 2 * PREP):
                        tile(t, t % 2, t // 2 + 1, P, jobs=t - 2 * EARLY - PREP)
                    dve.wait_ge(s_et, NJ + 3)
                    dve.tensor_scalar(bad[0:1, 0:1], psE[0:1, 0:1], 0.5, None, ALU.is_gt)
                    with dve.Fori(EARLY + PREP, NT // 2 - 1) as i:
                        for s in range(2):
                            tile(2 * i + s, s, i + 1, P)
                    tile(NT - 3, 0, NT // 2, P, TAIL)
                    tile(NT - 2, 1, 0, TAIL, 0)
                    for k in range(PAIRS):
                        t_low(NT - 1, 0, k, TAIL)

                @block.gpsimd
                def _(pool):
                    n = [0]

                    def link(ins):
                        n[0] += 1
                        ins.then_inc(s_p, 1)
                        pool.wait_ge(s_p, n[0])

                    link(nc.gpsimd.memset(ident[:, :], 0.0))
                    link(nc.gpsimd.affine_select(out=ident[:, :], in_=ident[:, :], compare_op=ALU.not_equal, fill=1.0,
                                                 base=0, pattern=[[-1, P]], channel_multiplier=1))
                    nc.gpsimd.memset(e_w[:, CH - 1, :], 0.0).then_inc(s_wpad, 1)
                    nc.gpsimd.memset(ones[:, :], 1.0)
                    nc.gpsimd.iota(iota2[:, :, :], pattern=[[0, 2], [1, W]], base=0, channel_multiplier=0,
                                   allow_small_or_imprecise_dtypes=True)
                    pool.wait_ge(s_edge, 16 * NEDGE)
                    link(nc.gpsimd.tensor_scalar(e_row[:, :, :], e_src[:, :, :], float(R), None, ALU.mult))
                    link(nc.gpsimd.tensor_copy(e_node[:, :, :], e_typ[:, :, :]))
                    link(nc.gpsimd.tensor_tensor(e_row[:, :, :], e_row[:, :, :], e_node[:, :, :], ALU.add))
                    nc.gpsimd.tensor_copy(e_node[:, :, :], e_dst[:, :, :]).then_inc(s_node, 1)
                    pool.wait_ge(s_par, 16 * NPAR)
                    nc.gpsimd.tensor_copy(boh[:, :], bor[:, :]).then_inc(s_bo, 1)
                    link(nc.gpsimd.tensor_copy(Wr2[:, :, 0, :], wrr[:, :, :]))
                    nc.gpsimd.tensor_tensor(Wr2[:, :, 1, :], wrr[:, :, :], Wr2[:, :, 0, :], ALU.subtract)
                    pool.wait_ge(s_bo, 1)
                    nc.gpsimd.tensor_tensor(bol[:, :], bor[:, :], boh[:, :], ALU.subtract).then_inc(s_bo, 1)

                    def load(j):
                        _, _, a, e = ffn[j]
                        pool.dma_start(fraw[:, j % 2, :, :], a[e, :, :].rearrange("(k p) n -> p k n", p=P))\
                            .then_inc(s_fl[j % 2], 16)

                    load(0)
                    for j, (hi, lo, _, e) in enumerate(ffn):
                        if j + 1 < len(ffn):
                            if j >= 1:
                                pool.wait_ge(s_fd, 2 * j)
                            load(j + 1)
                        pool.wait_ge(s_fl[j % 2], 16 * (j // 2 + 1))
                        nc.gpsimd.tensor_copy(hi[:, e, :, :], fraw[:, j % 2, :, :]).then_inc(s_fd, 1)
                        pool.wait_ge(s_fd, 2 * j + 1)
                        nc.gpsimd.tensor_tensor(lo[:, e, :, :], fraw[:, j % 2, :, :], hi[:, e, :, :],
                                                ALU.subtract).then_inc(s_fd, 1)

                @block.tensor
                def _(pe):
                    def transpose_x(t, s, rows):
                        pe.wait_ge(s_xn, t + 1)
                        if not (isinstance(t, int) and t == 0):
                            pe.wait_ge(s_xl, t)
                        for h in range(KH):
                            last = nc.tensor.transpose(psT[0][:, h, 0:rows], xn[0:rows, s, h * P:(h + 1) * P],
                                                       ident[0:rows, 0:rows])
                        last.then_inc(s_tr, 1)

                    def messages(t, s, k, rows):
                        if k == 0:
                            pe.wait_ge(s_xl, t + 1)
                        if isinstance(t, int) and t == 0:
                            pe.wait_ge(s_wgd, 2 * k + 2)
                        else:
                            pe.wait_ge(s_tl, PAIRS * t + k - 3)
                        n = 0
                        for h in range(KH):
                            for a, b in ((xTh, Wgh), (xTh, Wgl), (xTl, Wgh)):
                                last = nc.tensor.matmul(psP[k][0:rows, :, :], a[:, s, h, 0:rows], b[:, h, 2 * k:2 * k + 2, :],
                                                        start=(n == 0), stop=(n == 5))
                                n += 1
                        last.then_inc(s_mm, 1)

                    def turn_edges(n):
                        if n == 0:
                            pe.wait_ge(s_ep, 1)
                        else:
                            pe.wait_ge(s_ee, n)
                        if n < NJ:
                            q, c = edge_jobs[n]
                            part = (e_row, e_rel, e_w, e_node)[q]
                            for i in range(GT):
                                last = nc.tensor.transpose(psE[:, CG * i:CG * (i + 1)], part[:, c, i * P:(i + 1) * P],
                                                           ident[0:CG, 0:CG])
                        elif n == NJ:
                            for c in range(CH):
                                last = nc.tensor.transpose(psE[0:1, CG * c:CG * (c + 1)], gmin[:, c:c + 1],
                                                           ident[0:CG, 0:CG])
                        elif n == NJ + 1:
                            pe.wait_ge(s_bn, 12)
                            for q in range(4):
                                last = nc.tensor.transpose(psE[:, 2 * X * q:2 * X * (q + 1)],
                                                           praw[:, (0, 2, 5, 7)[q], :], ident[0:2 * X, 0:2 * X])
                        else:
                            last = nc.tensor.matmul(psE[:, 0:2], ones[0:CG, :], vio2[:, :], start=True, stop=True)
                        last.then_inc(s_et, 1)

                    def tile(t, s, rows_next, jobs=None):
                        for k in range(PAIRS):
                            messages(t, s, k, P)
                            if k == 1:
                                transpose_x(t + 1, 1 - s, rows_next)
                            if jobs is not None and PAIRS * jobs + k < NJ + 3:
                                turn_edges(PAIRS * jobs + k)

                    pe.wait_ge(s_p, 2)
                    transpose_x(0, 0, P)
                    tile(0, 0, P)
                    tile(1, 1, P)
                    with pe.Fori(1, EARLY) as i:
                        for s in range(2):
                            tile(2 * i + s, s, P)
                    for t in range(2 * EARLY, 2 * EARLY + PREP):
                        tile(t, t % 2, P)
                    for t in range(2 * EARLY + PREP, 2 * EARLY + 2 * PREP):
                        tile(t, t % 2, P, jobs=t - 2 * EARLY - PREP)
                    with pe.Fori(EARLY + PREP, NT // 2 - 1) as i:
                        for s in range(2):
                            tile(2 * i + s, s, P)
                    tile(NT - 3, 0, P)
                    tile(NT - 2, 1, TAIL)
                    for k in range(PAIRS):
                        messages(NT - 1, 0, k, TAIL)

        sumT = sb("sumT", [P, KH, NP], f32)
        B = ExitStack()
        with B:
            rows3, gat3 = sb("rows3", [P, GT], i32, B), sb("gat3", [P, GT, 2 * D], f16, B)
            sel3 = sb("sel3", [P, GT, 2, WS], f16, B)
            iotaW = sb("iotaW", [P, 2, WS], f16, B)
            relw = sb("relw", [P, GT], f32, B)
            nodeB, idxB = sb("nodeB", [P, COLS], f32, B), sb("idxB", [P, COLS], i32, B)
            psW = [B.enter_context(nc.psum_tensor(f"psW{h}", [P, 2, WS], f32)) for h in range(KH)]
            z_iota, z_clear = sem("wide_iota", B), sem("sums_cleared", B)
            z_node, z_idx = sem("nodes_loaded", B), sem("rows_loaded", B)
            z_rows, z_gat = sem("rows_staged", B), sem("wide_gathered", B)
            z_sel, z_dve, z_mm = sem("wide_selected", B), sem("wide_chain", B), sem("wide_product", B)

            with nc.Block() as block:
                @block.gpsimd
                def _(pool):
                    nc.gpsimd.iota(iotaW[:, :, :], pattern=[[0, 2], [1, WS]], base=0, channel_multiplier=0,
                                   allow_small_or_imprecise_dtypes=True).then_inc(z_iota, 1)
                    flag = pool.value_load(bad[0:1, 0:1], min_val=0, max_val=1)
                    with pool.If(flag == 1):
                        pool.dma_start(nodeB[:, :], nodes).then_inc(z_node, 16)
                        pool.dma_start(idxB[:, :], rows_of).then_inc(z_idx, 16)
                        pool.wait_ge(z_idx, 16)
                        with pool.Fori(0, NG) as g:
                            pool.wait_ge(z_mm, NW * g + 1)
                            nc.gpsimd.tensor_copy(rows3[:, :], idxB[:, ds(GT * g, GT)]).then_inc(z_rows, 1)
                            pool.wait_ge(z_rows, 2 * g + 1)
                            pool.sem_inc(z_rows, 1)
                            for i in range(GT):
                                pool.indirect_dma_start(out=gat3[:, i, :], out_offset=None, in_=table,
                                                        in_offset=bass.IndirectOffsetOnAxis(ap=rows3[:, i:i + 1], axis=0))\
                                    .then_inc(z_gat, 16)

                @block.vector
                def _(dve):
                    flag = dve.value_load(bad[0:1, 0:1], min_val=0, max_val=1)
                    with dve.If(flag == 1):
                        dve.memset(sumT[:, :, :], 0.0).then_inc(z_clear, 1)
                        dve.wait_ge(z_iota, 1)
                        dve.wait_ge(z_clear, 1)
                        dve.wait_ge(z_node, 16)
                        C = 3 * NW + 1
                        with dve.Fori(0, NG) as g:
                            dve.tensor_copy(relw[:, :], nodeB[:, ds(GT * g, GT)]).then_inc(z_dve, 1)
                            with dve.Fori(0, NW) as w:
                                dve.wait_ge(z_dve, C * g + 3 * w + 1)
                                for i in range(GT):
                                    last = dve.scalar_tensor_tensor(
                                        sel3[:, i, :, :], iotaW[:, :, :], relw[:, i:i + 1],
                                        wp[:, ds(GT * g + i, 1), :].rearrange("p a c -> p (a c)").unsqueeze(2)
                                        .to_broadcast([P, 2, WS]), ALU.is_equal, ALU.mult)
                                last.then_inc(z_sel, 1)
                                dve.wait_ge(z_sel, NW * g + w + 1)
                                dve.tensor_scalar(relw[:, :], relw[:, :], float(WS), None, ALU.subtract).then_inc(z_dve, 1)
                                dve.wait_ge(z_mm, NW * g + w + 2)
                                for part in range(2):
                                    if part == 1:
                                        dve.wait_ge(z_dve, C * g + 3 * w + 3)
                                    for h in range(KH):
                                        last = dve.tensor_tensor(sumT[:, h, ds(w * WS, WS)], sumT[:, h, ds(w * WS, WS)],
                                                                 psW[h][:, part, :], ALU.add)
                                    last.then_inc(z_dve, 1)
                        dve.wait_ge(z_dve, C * NG)
                        dve.memset(wp[:, :, :], 0.0)

                @block.tensor
                def _(pe):
                    flag = pe.value_load(bad[0:1, 0:1], min_val=0, max_val=1)
                    with pe.If(flag == 1):
                        pe.sem_inc(z_mm, 1)
                        with pe.Fori(0, NG) as g:
                            with pe.Fori(0, NW) as w:
                                pe.wait_ge(z_gat, 16 * GT * (g + 1))
                                pe.wait_ge(z_sel, NW * g + w + 1)
                                for h in range(KH):
                                    for i in range(GT):
                                        nc.tensor.matmul(psW[h][:, :, :], gat3[:, i, h * P:(h + 1) * P], sel3[:, i, :, :],
                                                         start=(i == 0), stop=False)
                                        last = nc.tensor.matmul(psW[h][:, 0, :], gat3[:, i, D + h * P:D + (h + 1) * P],
                                                                sel3[:, i, 0, :], start=False, stop=(i == GT - 1))
                                last.then_inc(z_mm, 1)

        C = ExitStack()
        with C:
            gat = sb("gat", [P, SLOTS, 2 * D], f16, C)
            sel = sb("sel", [P, SS, GT, 2, W], f16, C)
            HG = (GB + 1) // 2
            rowsA, rowsB = sb("rowsA", [P, GT * HG], i32, C), sb("rowsB", [P, GT * (GB - HG)], i32, C)
            rowsP = sb("rowsP", [P, GT * PRO], i32, C)
            aggT = sb("aggT", [P, KH, BT], f32, C)
            xn2 = aggT[:, :, :].rearrange("p h c -> p (h c)").rearrange("p (q d) -> p q d", d=D)
            x1, acc = sb("x1", [P, QT, D], f32, C), sb("acc", [P, QT, D], f32, C)
            xh, xl = sb("xh", [P, KH, BT], f32r, C), sb("xl", [P, KH, BT], f32r, C)
            act32 = sb("act32", [P, KH, BT], f32, C)
            h1h, h1l = sb("h1h", [P, KH, BT], f32r, C), sb("h1l", [P, KH, BT], f32r, C)
            h2h, h2l = sb("h2h", [P, KH, BT], f32r, C), sb("h2l", [P, KH, BT], f32r, C)
            bst, bmv = sb("bst", [P, QT, 6], f32, C), sb("bmv", [P, QT, 2], f32, C)
            dev, inv = sb("dev", [P, QT, 1], f32, C), sb("inv", [P, QT, 1], f32, C)
            lg, lgm, ex = sb("lg", [P, QT, X], f32, C), sb("lgm", [P, QT, X], f32, C), sb("ex", [P, QT, X], f32, C)
            spare = sb("spare", [P, 1], f32, C)
            mx, sm = sb("mx", [P, QT], f32, C), sb("sm", [P, QT], f32, C)
            rw = sb("rw", [P, QT, X], f32, C)
            rw24 = sb("rw24", [P, QT, 3 * X], f32r, C)
            rwT = sb("rwT", [3 * X, QT, P], f32r, C)
            psH = [C.enter_context(nc.psum_tensor(f"psH{i}", [P, 512], f32)) for i in range(HB)]
            psY = [C.enter_context(nc.psum_tensor(f"psY{i}", [P, D], f32)) for i in range(QT)]
            psA = C.enter_context(nc.psum_tensor("psA", [P, KH, 2, W], f32))
            psM = C.enter_context(nc.psum_tensor("psM", [P, 512], f32))

            c_gat = [sem(f"gathered{i}", C) for i in range(SLOTS)]
            c_x1T, c_x1 = sem("second_part_transposed", C), sem("second_part_split", C)
            c_lg = sem("logits_low", C)
            c_zero = sem("zeros_set", C)
            c_clear = sem("sums_cleared2", C)
            c_freed = sem("slots_freed", C)
            c_rowsP, c_rows = sem("first_rows_loaded", C), [sem(f"rows_loaded{k}", C) for k in range(2)]
            c_sel = sem("selected", C)
            c_sum, c_add1, c_added = sem("group_product", C), sem("group_added_high", C), sem("group_added", C)
            c_agg = sem("block_sums_read", C)
            c_mm, c_act, c_lo = sem("layer_product", C), sem("activated", C), sem("activation_split", C)
            c_y, c_yd = sem("expert_output", C), sem("output_added", C)
            c_m, c_mr = sem("misc_bank_written", C), sem("misc_bank_read", C)
            c_x, c_out = sem("residual_loaded", C), sem("block_stored", C)
            c_st, c_dev, c_xn = sem("norm_chain", C), sem("deviation_ready", C), sem("x_normed2", C)
            c_xh = sem("xT_high2", C)
            c_r, c_ex, c_rw = sem("router_chain", C), sem("router_exp", C), sem("router_weights_split", C)

            def block_and_expert(t, e):
                return (t + 1, 0) if e == X else (t, e)

            def unit(t, l, e, o):
                return 2 * KH * (X * t + e) + KH * l + o

            def hidden_bank(l, e, o):
                n, per_block = KH * (2 * e + l) + o, 2 * KH * X
                last = next(k for k in range(1, per_block) if (n - k) % per_block % HB == n % HB)
                return psH[n % HB], last

            def is_head(t):
                return isinstance(t, int) and t == 0

            def tiles(t):
                return 1 if is_head(t) else QT

            def rows(t):
                return HEAD if is_head(t) else P

            def width(t):
                return HEAD if is_head(t) else BT

            def hidden_width(t):
                return HIDDEN if is_head(t) else BT

            def first(t):
                return 0 if is_head(t) else HEAD + BT * (t - 1)

            def token_tiles(x, a, b, r):
                if r < P:
                    return x[:, :, a * P:a * P + r].unsqueeze(1)
                return x[:, :, a * P:b * P].rearrange("p h (q c) -> p q h c", c=P)

            def bank_tiles(bank, a, b, r):
                return bank[:, 0:(b - a) * D].rearrange("p (q h c) -> p q h c", h=KH, c=P)[:, :, :, 0:r]

            def y_before(t):
                return 0 if is_head(t) else 9 * QT * t + 9 * (1 - QT)

            def m_before(t):
                return 5 * t + 2

            def m_of(t, use, part=0):
                if t is None:
                    return {"residual": 0, "xT": 1}[use]
                return m_before(t) + {"route": 0, "turn": 1, "residual": 2, "xT": 4}[use] + part

            def part_of(t, part):
                return (0, 1) if t is None else ((0, 2), (2, QT))[part]

            def xT_before(t):
                return 1 + QT * t

            def chain_before(t):
                return 0 if is_head(t) else 4 + (3 * QT + 1) * (t - 1)

            def schedule(t, ng, ahead):
                s, k, left = [], tiles(t), list(range(ng))
                at = {}

                def put(*step):
                    s.append(step)
                    for more in at.pop(step, ()):
                        put(*more)

                def group():
                    if left:
                        put("sum", left.pop(0))

                at["mid", 0, KH - 1] = [("weights",)]
                at["down", 0, k - 1] = [("turn",)]
                if ahead:
                    at["up", READ + 1, KH - 1] = [("read",)]
                    at["mid", READ + 1, 0] = [("residual", 1)]
                    at["up", READ + 2, KH - 1] = [("deviation",), ("scale",)]
                at["up", BIAS + 1, KH - 1] = [("bias", 2)] if k == QT else []
                at["mid", BIAS, KH - 1] = [("bias", 1)] if k == QT else []
                put("route",)
                group()
                for e in range(X):
                    for o in range(KH):
                        put("mid", e, o)
                    group()
                    if e + 1 < X or ahead:
                        for o in range(KH):
                            put("up", e + 1, o)
                    for q in range(k):
                        put("down", e, q)
                    group()
                    if e == BIAS - 1:
                        put("bias", 0)
                    if e == READ and ahead:
                        put("residual", 0)
                    if e == READ + 1 and ahead:
                        put("xT", 0)
                        put("xT", 1)
                while left:
                    group()
                assert not at
                return s

            def vector_order(s):
                v, n = [], 0

                def sums(step):
                    return ([("select", step[1])], [("add", step[1])]) if step and step[0] == "sum" else ([], [])

                while n < len(s):
                    if s[n][0] == "mid":
                        end = next(i for i in range(n, len(s)) if s[i][0] in ("sum", "up", "down"))
                        select, add = sums(s[end])
                        between = [x for x in s[n:end] if x[0] == "xT"]
                        behind = [x for x in s[n:end] if x[0] not in ("mid", "xT")]
                        v += [*select, s[n], *between, *add, ("mid", s[n][1], KH - 1), *behind]
                        n = end + len(add)
                    elif s[n][0] in ("up", "down"):
                        end = next((i for i in range(n, len(s)) if s[i][0] in ("mid", "sum")), len(s))
                        select, add = sums(s[end] if end < len(s) else None)
                        up = [x for x in s[n:end] if x[0] == "up"]
                        scale = [x for x in s[n:end] if x[0] == "scale"]
                        rest = [x for x in s[n:end] if x not in up + scale]
                        first = rest.index(next(x for x in rest if x[0] == "down")) + 1
                        behind_weights = bool(v) and v[-1] == ("weights",)
                        if scale:
                            v += [up[0], *rest[:first], *scale, up[1], *rest[first:], *select, *add]
                        else:
                            sooner, later = ([], select) if behind_weights else (select, [])
                            v += [*sooner, *up[:1], *rest[:first], *up[1:], *later, *rest[first:], *add]
                        n = end + len(add)
                    elif s[n][0] == "sum":
                        v += [*sums(s[n])[0], *sums(s[n])[1]]
                        n += 1
                    else:
                        v.append(s[n])
                        n += 1
                return v

            def out_slot(e):
                return BIAS if e is None else e + (e >= BIAS)

            PT = GT * PRO

            def slot_pro(i):
                return (i + SLOTS - PT % SLOTS) % SLOTS

            pro_uses = [sum(slot_pro(i) == s for i in range(PT)) for s in range(SLOTS)]
            blk_uses = [sum(i % SLOTS == s for i in range(GT * GB)) for s in range(SLOTS)]

            def group_slots(t, j):
                if t is None:
                    got = [(slot_pro(i), sum(slot_pro(k) == slot_pro(i) for k in range(i + 1)))
                           for i in range(GT * j, GT * (j + 1))]
                else:
                    got = [(i % SLOTS, pro_uses[i % SLOTS] + blk_uses[i % SLOTS] * t + i // SLOTS + 1)
                           for i in range(GT * j, GT * (j + 1))]
                return got, (j if t is not None else j - PRO) % SS

            def group_number(t, j):
                return j if t is None else PRO + GB * t + j

            def after(t, j, k):
                n = group_number(t, j) + k if not isinstance(t, (int, type(None))) else None
                if n is not None:
                    return (t, j + k) if j + k < GB else (t + 1, j + k - GB)
                n = group_number(t, j) + k
                if n >= NG:
                    return None
                return (None, n) if n < PRO else ((n - PRO) // GB, (n - PRO) % GB)

            def run(eng, step):
                step(0, groups_of(0), True)
                with eng.Fori(1, LAST - 1) as t:
                    step(t, GB, True)
                step(LAST - 1, groups_of(LAST - 1), True)
                step(LAST, groups_of(LAST), False)

            with nc.Block() as block:
                @block.sync
                def _(sp):
                    sp.dma_start(rowsP[:, :], rows_of[:, 0:GT * PRO]).then_inc(c_rowsP, 16)

                    def load_rows(t, k):
                        lo, hi = ((0, HG), (HG, GB))[k]
                        n = min(hi, groups_of(t) if isinstance(t, int) else GB) - lo
                        if n > 0:
                            if not is_head(t):
                                sp.wait_ge(c_sum, group_number(t, hi - GB))
                            sp.dma_start((rowsA, rowsB)[k][:, 0:GT * n],
                                         rows_of[:, ds(GT * group_number(t, lo), GT * n)]).then_inc(c_rows[k], 16)

                    load_rows(0, 0)
                    load_rows(0, 1)
                    sp.dma_start(x1[0:HEAD, 0, :], x[0:HEAD, :]).then_inc(c_x, 16)

                    def step(t, ng, ahead):
                        if ahead:
                            sp.wait_ge(c_yd, y_before(t) + tiles(t))
                            sp.dma_start(x1[:, :, :], x[ds(first(t + 1), BT), :].rearrange("(q p) c -> p q c", p=P))\
                              .then_inc(c_x, 16)
                            load_rows(t + 1, 0)
                        sp.wait_ge(c_yd, y_before(t) + 9 * tiles(t))
                        if is_head(t):
                            sp.dma_start(out[0:HEAD, :], acc[0:HEAD, 0, :]).then_inc(c_out, 16)
                        else:
                            sp.dma_start(out[ds(first(t), BT), :].rearrange("(q p) c -> p q c", p=P), acc[:, :, :])\
                              .then_inc(c_out, 16)
                        if ahead:
                            load_rows(t + 1, 1)

                    step(0, GB, True)
                    with sp.Fori(1, LAST - 2) as t:
                        step(t, GB, True)
                    for t in range(LAST - 2, LAST + 1):
                        step(t, groups_of(t), t < LAST)
                    sp.wait_ge(c_out, 16 * (LAST + 1))

                @block.gpsimd
                def _(pool):
                    def gather(t, j, ap):
                        got, _ = group_slots(t, j)
                        if not (t is None and j < 5):
                            pool.wait_ge(c_sum, group_number(t, j) - 4)
                            pool.sem_inc(c_freed, 1)
                        for i, (slot, _) in enumerate(got):
                            pool.indirect_dma_start(out=gat[:, slot, :], out_offset=None, in_=table,
                                                    in_offset=bass.IndirectOffsetOnAxis(ap=ap[:, i:i + 1], axis=0))\
                                .then_inc(c_gat[slot], 16)

                    pool.wait_ge(c_rowsP, 16)
                    for j in range(PRO):
                        gather(None, j, rowsP[:, GT * j:GT * (j + 1)])

                    def step(t, ng, ahead):
                        for k, (stage_t, lo, hi) in enumerate(((rowsA, 0, HG), (rowsB, HG, GB))):
                            if lo >= ng:
                                continue
                            pool.wait_ge(c_rows[k], 16 * (t + 1))
                            for j in range(lo, min(hi, ng)):
                                gather(t, j, stage_t[:, GT * (j - lo):GT * (j - lo + 1)])

                    run(pool, step)

                @block.scalar
                def _(act):
                    def read_block(t):
                        nxt = 0 if t is None else t + 1
                        act.wait_ge(c_added, LEAD if t is None else PRO + GB * t + min(JP, GB if not isinstance(t, int) else groups_of(t)))
                        nc.scalar.activation(aggT[:, :, 0:width(nxt)], sumT[:, :, ds(first(nxt), width(nxt))], ACT.Relu)\
                            .then_inc(c_agg, 1)
                        nc.scalar.activation(spare[:, :], eps[:, :], ACT.Sqrt)

                    def deviation(t):
                        nxt = 0 if t is None else t + 1
                        r, q = rows(nxt), tiles(nxt)
                        act.wait_ge(c_st, chain_before(nxt) + 3 * q)
                        nc.scalar.activation(dev[0:r, 0:q, :], bmv[0:r, 0:q, 1:2], ACT.Sqrt, bias=eps[0:r, 0:1])\
                            .then_inc(c_dev, 1)

                    def xT(t, part):
                        nxt = 0 if t is None else t + 1
                        r, (a, b) = rows(nxt), part_of(t, part)
                        if part == 0:
                            act.wait_ge(c_m, m_of(t, "xT") + 1)
                        else:
                            act.wait_ge(c_x1T, t + 1)
                        nc.scalar.copy(token_tiles(xh, a, b, r), bank_tiles((psM, psY[0])[part], a, b, r))\
                            .then_inc(c_xh, 1)

                    def layer(t, l, e, o):
                        t, e = block_and_expert(t, e)
                        w, u = hidden_width(t), unit(t, l, e, o)
                        hi, ps = (h1h, h2h)[l], hidden_bank(l, e, o)[0]
                        scale_ap, shift_ap = (bnp[:, 2 * l + k, KH * e + o:KH * e + o + 1] for k in range(2))
                        act.wait_ge(c_mm, u + 1)
                        nc.scalar.activation(hi[:, o, 0:w], ps[:, 0:w], ACT.Relu, bias=shift_ap, scale=scale_ap)
                        if not (is_head(t) and e == 0 and l == 0):
                            act.wait_ge(c_lo, u - 1)
                        nc.scalar.activation(act32[:, o, 0:w], ps[:, 0:w], ACT.Relu, bias=shift_ap, scale=scale_ap)\
                            .then_inc(c_act, 1)

                    flag = act.value_load(bad[0:1, 0:1], min_val=0, max_val=1)
                    with act.If(flag == 0):
                        nc.scalar.activation(sumT[:, 1, :], eps[:, 0:1].to_broadcast([P, NP]), ACT.Copy, scale=0.0)\
                            .then_inc(c_clear, 1)
                    with act.If(flag == 1):
                        act.sem_inc(c_clear, 1)
                    read_block(None)
                    deviation(None)
                    xT(None, 0)
                    for o in range(KH):
                        layer(0, 0, 0, o)

                    def step(t, ng, ahead):
                        for kind, *n in schedule(t, ng, ahead):
                            if kind == "up":
                                layer(t, 0, *n)
                            elif kind == "mid":
                                layer(t, 1, *n)
                            elif kind == "route":
                                act.wait_ge(c_r, 3 * t + 2)
                                r = rows(t)
                                nc.scalar.activation(ex[0:r, 0:tiles(t), :], lgm[0:r, 0:tiles(t), :], ACT.Exp).then_inc(c_ex, 1)
                            elif kind == "turn":
                                act.wait_ge(c_m, m_of(t, "turn") + 1)
                                nc.scalar.copy(rwT[:, 0:tiles(t), 0:rows(t)],
                                               psM[0:3 * X, 0:tiles(t) * P].rearrange("p (q c) -> p q c", c=P)
                                               [:, :, 0:rows(t)]).then_inc(c_mr, 1)
                            elif kind == "read":
                                read_block(t)
                            elif kind == "deviation":
                                deviation(t)
                            elif kind == "xT":
                                xT(t, *n)

                    run(act, step)

                @block.vector
                def _(dve):
                    regs = [dve.alloc_register(f"window{j}") for j in range(GB)]

                    def select(t, j):
                        g = group_number(t, j)
                        slot = group_slots(t, j)[1]
                        if not (t is None and j < SS):
                            dve.wait_ge(c_sum, g - 4)
                        for i in range(GT):
                            col = GT * g + i
                            last = dve.scalar_tensor_tensor(
                                sel[:, slot, i, :, :], iota2[:, :, :], rel[:, ds(col, 1)],
                                wp[:, ds(col, 1), :].rearrange("p a c -> p (a c)").unsqueeze(2).to_broadcast([P, 2, W]),
                                ALU.is_equal, ALU.mult)
                        last.then_inc(c_sel, 1)

                    def add(t, j):
                        g = group_number(t, j)
                        at = dve.snap(regs[j], min_val=0, max_val=N - 1)
                        dve.wait_ge(c_sum, g + 1)
                        if t is None and j == 0:
                            dve.wait_ge(c_clear, 2)
                        else:
                            dve.wait_ge(c_added, g)
                        dve.tensor_tensor(sumT[:, :, ds(at, W)], sumT[:, :, ds(at, W)], psA[:, :, 0, :], ALU.add)\
                           .then_inc(c_add1, 1)
                        dve.wait_ge(c_add1, g + 1)
                        dve.tensor_tensor(sumT[:, :, ds(at, W)], sumT[:, :, ds(at, W)], psA[:, :, 1, :], ALU.add)\
                           .then_inc(c_added, 1)

                    def select_behind(t, j):
                        nxt = after(t, j, 2)
                        if nxt is not None:
                            select(*nxt)

                    def sum_group(t, j):
                        select_behind(t, j)
                        add(t, j)

                    def residual(t, part):
                        nxt = 0 if t is None else t + 1
                        r, (a, b) = rows(nxt), part_of(t, part)
                        m = m_of(t, "residual", part)
                        dve.wait_ge(c_x, 16 * (nxt + 1))
                        dve.wait_ge(c_m, m + 1)
                        dve.tensor_tensor(x1[0:r, a:b, :], x1[0:r, a:b, :],
                                          psM[0:r, 0:(b - a) * D].rearrange("p (q d) -> p q d", d=D), ALU.add)\
                           .then_inc(c_mr, 1)
                        dve.wait_ge(c_mr, m + 1)
                        for q in range(a, b):
                            c = chain_before(nxt) + 3 * q
                            dve.bn_stats(bst[0:r, q, :], x1[0:r, q, :]).then_inc(c_st, 1)
                            dve.wait_ge(c_st, c + 1)
                            dve.sem_inc(c_st, 1)
                            dve.bn_aggr(bmv[0:r, q, :], bst[0:r, q, :]).then_inc(c_st, 1)

                    def scale(t):
                        nxt = 0 if t is None else t + 1
                        r, k = rows(nxt), tiles(nxt)
                        dve.wait_ge(c_dev, nxt + 1)
                        dve.reciprocal(inv[0:r, 0:k, :], dev[0:r, 0:k, :]).then_inc(c_st, 1)
                        dve.wait_ge(c_st, chain_before(nxt) + 3 * k + 1)
                        for q in range(k):
                            dve.tensor_scalar(xn2[0:r, q, :], x1[0:r, q, :], bmv[0:r, q, 0:1], inv[0:r, q, :],
                                              ALU.subtract, ALU.mult).then_inc(c_xn, 1)

                    def xT(t, part):
                        nxt = 0 if t is None else t + 1
                        r, (a, b) = rows(nxt), part_of(t, part)
                        dve.wait_ge(c_xh, 1 if t is None else 2 * t + part + 2)
                        dve.tensor_tensor(token_tiles(xl, a, b, r), bank_tiles((psM, psY[0])[part], a, b, r),
                                          token_tiles(xh, a, b, r), ALU.subtract).then_inc((c_mr, c_x1)[part], 1)

                    def route(t):
                        r, k = rows(t), tiles(t)
                        dve.wait_ge(c_m, m_before(t) + 1)
                        parts = psM[0:r, 0:k * 2 * X].rearrange("p (q a e) -> p q a e", a=2, e=X)
                        dve.tensor_tensor(lg[0:r, 0:k, :], parts[:, :, 1, :],
                                          brb[0:r, :].unsqueeze(1).to_broadcast([r, k, X]), ALU.add).then_inc(c_lg, 1)
                        dve.wait_ge(c_lg, t + 1)
                        dve.tensor_tensor(lg[0:r, 0:k, :], parts[:, :, 0, :], lg[0:r, 0:k, :], ALU.add).then_inc(c_mr, 1)
                        dve.wait_ge(c_mr, m_before(t) + 1)
                        dve.tensor_reduce(mx[0:r, 0:k], lg[0:r, 0:k, :], AX.X, ALU.max).then_inc(c_r, 1)
                        dve.wait_ge(c_r, 3 * t + 1)
                        dve.tensor_tensor(lgm[0:r, 0:k, :], lg[0:r, 0:k, :], mx[0:r, 0:k].unsqueeze(2).to_broadcast([r, k, X]),
                                          ALU.subtract).then_inc(c_r, 1)

                    def weights(t):
                        r, k = rows(t), tiles(t)
                        dve.wait_ge(c_ex, t + 1)
                        dve.tensor_reduce(sm[0:r, 0:k], ex[0:r, 0:k, :], AX.X, ALU.add).then_inc(c_r, 1)
                        dve.wait_ge(c_r, 3 * t + 3)
                        dve.reciprocal(mx[0:r, 0:k], sm[0:r, 0:k]).then_inc(c_rw, 1)
                        dve.wait_ge(c_rw, 4 * t + 1)
                        dve.tensor_tensor(rw[0:r, 0:k, :], ex[0:r, 0:k, :], mx[0:r, 0:k].unsqueeze(2).to_broadcast([r, k, X]),
                                          ALU.mult).then_inc(c_rw, 1)
                        dve.wait_ge(c_rw, 4 * t + 2)
                        dve.tensor_copy(rw24[0:r, 0:k, 0:X], rw[0:r, 0:k, :])
                        dve.tensor_copy(rw24[0:r, 0:k, 2 * X:3 * X], rw[0:r, 0:k, :]).then_inc(c_rw, 1)
                        dve.wait_ge(c_rw, 4 * t + 3)
                        dve.tensor_tensor(rw24[0:r, 0:k, X:2 * X], rw[0:r, 0:k, :], rw24[0:r, 0:k, 0:X], ALU.subtract)\
                           .then_inc(c_rw, 1)

                    def layer(t, l, e, o):
                        t, e = block_and_expert(t, e)
                        w, u = hidden_width(t), unit(t, l, e, o)
                        hi, lo = ((h1h, h1l), (h2h, h2l))[l]
                        dve.wait_ge(c_act, u + 1)
                        dve.tensor_tensor(lo[:, o, 0:w], act32[:, o, 0:w], hi[:, o, 0:w], ALU.subtract).then_inc(c_lo, 1)

                    def down(t, e, q):
                        r, v = rows(t), out_slot(e) * tiles(t) + q
                        dve.wait_ge(c_y, y_before(t) + v + 1)
                        if e == 0 and q == 0 and not is_head(t):
                            dve.wait_ge(c_out, 16 * t)
                        if e != 0:
                            dve.wait_ge(c_yd, y_before(t) + v - tiles(t) + 1)
                        if e is None:
                            dve.tensor_tensor(acc[0:r, q, :], acc[0:r, q, :], psY[q][0:r, :], ALU.add)\
                               .then_inc(c_yd, 1)
                        else:
                            dve.scalar_tensor_tensor(acc[0:r, q, :], psY[q][0:r, :], rw[0:r, q, e:e + 1],
                                                     (acc if e else x1)[0:r, q, :], ALU.mult, ALU.add).then_inc(c_yd, 1)

                    flag = dve.value_load(bad[0:1, 0:1], min_val=0, max_val=1)
                    with dve.If(flag == 0):
                        dve.memset(sumT[:, 0, :], 0.0).then_inc(c_clear, 1)
                    with dve.If(flag == 1):
                        dve.sem_inc(c_clear, 1)
                    dve.memset(act32[:, :, HEAD:HIDDEN], 0.0).then_inc(c_zero, 1)
                    dve.wait_ge(c_zero, 1)
                    for x_part in (xh, xl):
                        dve.tensor_copy(x_part[:, :, HEAD:HIDDEN], act32[:, :, HEAD:HIDDEN])
                    dve.load(regs[0:PRO], base[0:1, 0:PRO])
                    select(None, 0)
                    select(None, 1)
                    for j in range(LEAD):
                        sum_group(None, j)
                    residual(None, 0)
                    scale(None)
                    xT(None, 0)
                    layer(0, 0, 0, 0)
                    layer(0, 0, 0, 1)
                    for j in range(LEAD, PRO):
                        sum_group(None, j)

                    def step(t, ng, ahead):
                        if ng:
                            dve.load(regs[0:ng], base[0:1, ds(PRO + GB * t, ng)])
                        for kind, *n in vector_order(schedule(t, ng, ahead)):
                            if kind == "select":
                                select_behind(t, *n)
                            elif kind == "add":
                                add(t, *n)
                            elif kind == "route":
                                route(t)
                            elif kind == "weights":
                                weights(t)
                            elif kind == "up":
                                layer(t, 0, *n)
                            elif kind == "mid":
                                layer(t, 1, *n)
                            elif kind == "down":
                                down(t, *n)
                            elif kind == "bias":
                                down(t, None, *n)
                            elif kind == "residual":
                                residual(t, *n)
                            elif kind == "scale":
                                scale(t)
                            elif kind == "xT":
                                xT(t, *n)

                    run(dve, step)

                @block.tensor
                def _(pe):
                    def sum_group(t, j):
                        got, s = group_slots(t, j)
                        g = group_number(t, j)
                        if t is None and j == 0:
                            pe.wait_ge(c_sel, 1)
                        else:
                            pe.wait_ge(c_added, g)
                        for slot, count in got:
                            pe.wait_ge(c_gat[slot], 16 * count)
                        for h in range(KH):
                            for i, (slot, _) in enumerate(got):
                                nc.tensor.matmul(psA[:, h, :, :], gat[:, slot, h * P:(h + 1) * P], sel[:, s, i, :, :],
                                                 start=(i == 0), stop=False)
                                last = nc.tensor.matmul(psA[:, h, 0, :], gat[:, slot, D + h * P:D + (h + 1) * P],
                                                        sel[:, s, i, 0, :], start=False, stop=(i == GT - 1))
                        last.then_inc(c_sum, 1)

                    def misc_free(m):
                        if not (isinstance(m, int) and m == 0):
                            pe.wait_ge(c_mr, m)

                    def residual(t, part):
                        nxt = 0 if t is None else t + 1
                        r, (a, b) = rows(nxt), part_of(t, part)
                        pe.wait_ge(c_agg, nxt + 1)
                        misc_free(m_of(t, "residual", part))
                        for q in range(a, b):
                            for h in range(KH):
                                last = nc.tensor.transpose(psM[0:r, (q - a) * D + h * P:(q - a) * D + (h + 1) * P],
                                                           aggT[:, h, q * P:q * P + r], ident[:, :])
                        last.then_inc(c_m, 1)

                    def xT(t, part):
                        nxt = 0 if t is None else t + 1
                        r, (a, b) = rows(nxt), part_of(t, part)
                        pe.wait_ge(c_xn, 1 if t is None else xT_before(t) + b)
                        if part == 0:
                            misc_free(m_of(t, "xT"))
                        else:
                            pe.wait_ge(c_yd, y_before(t) + out_slot(READ + 1) * tiles(t) + 1)
                        for q in range(a, b):
                            for h in range(KH):
                                at = (q - a) * D + h * P
                                last = nc.tensor.transpose((psM, psY[0])[part][:, at:at + r],
                                                           xn2[0:r, q, h * P:(h + 1) * P], ident[0:r, 0:r])
                        last.then_inc((c_m, c_x1T)[part], 1)

                    def route(t):
                        r, k = rows(t), tiles(t)
                        misc_free(m_before(t))
                        for q in range(k):
                            for h in range(KH):
                                nc.tensor.matmul(psM[0:r, 2 * X * q:2 * X * (q + 1)], xh[:, h, q * P:q * P + r],
                                                 Wr2[:, h, :, :], start=(h == 0), stop=False)
                                last = nc.tensor.matmul(psM[0:r, 2 * X * q:2 * X * q + X], xl[:, h, q * P:q * P + r],
                                                        Wr2[:, h, 0, :], start=False, stop=(h == KH - 1))
                        last.then_inc(c_m, 1)

                    def turn(t):
                        r = rows(t)
                        pe.wait_ge(c_rw, 4 * t + 4)
                        misc_free(m_of(t, "turn"))
                        for q in range(tiles(t)):
                            last = nc.tensor.transpose(psM[0:3 * X, q * P:q * P + r], rw24[0:r, q, :].bitcast(f32),
                                                       ident[0:r, 0:r])
                        last.then_inc(c_m, 1)

                    def layer(t, l, e, o):
                        t, e = block_and_expert(t, e)
                        w, u = hidden_width(t), unit(t, l, e, o)
                        wh, wl = ((W1h, W1l), (W2h, W2l))[l]
                        hi, lo = ((xh, xl), (h1h, h1l))[l]
                        if o == 0:
                            if l == 1:
                                pe.wait_ge(c_lo, unit(t, 0, e, KH))
                            else:
                                pe.wait_ge(c_mr, m_before(t))
                                if e == 0 and not is_head(t):
                                    pe.wait_ge(c_x1, t)
                        ps, last_use = hidden_bank(l, e, o)
                        if not (is_head(t) and u < HB):
                            pe.wait_ge(c_act, u - last_use + 1)
                        n = 0
                        for h in range(KH):
                            for a, b in ((wh, hi), (wh, lo), (wl, hi)):
                                last = nc.tensor.matmul(ps[:, 0:w], a[:, e, h, o * P:(o + 1) * P],
                                                        b[:, h, 0:w], start=(n == 0), stop=(n == 5))
                                n += 1
                        last.then_inc(c_mm, 1)

                    def down(t, e, q):
                        r, v = rows(t), out_slot(e) * tiles(t) + q
                        if q == 0:
                            pe.wait_ge(c_lo, unit(t, 1, e, KH))
                        if e == BIAS:
                            pe.wait_ge(c_yd, y_before(t) + v - tiles(t) + 1)
                        n = 0
                        for h in range(KH):
                            for a, b in ((h2h, Woh), (h2h, Wol), (h2l, Woh)):
                                last = nc.tensor.matmul(psY[q][0:r, :], a[:, h, q * P:q * P + r], b[:, e, h, :],
                                                        start=(n == 0), stop=(n == 5))
                                n += 1
                        last.then_inc(c_y, 1)

                    def bias(t, q):
                        r, v = rows(t), out_slot(None) * tiles(t) + q
                        if q == 0:
                            pe.wait_ge(c_mr, m_of(t, "turn") + 1)
                        pe.wait_ge(c_yd, y_before(t) + v - tiles(t) + 1)
                        nc.tensor.matmul(psY[q][0:r, :], rwT[:, q, 0:r], bo24[:, :], start=True, stop=True)\
                          .then_inc(c_y, 1)

                    for j in range(LEAD):
                        sum_group(None, j)
                    residual(None, 0)
                    xT(None, 0)
                    layer(0, 0, 0, 0)
                    layer(0, 0, 0, 1)
                    for j in range(LEAD, PRO):
                        sum_group(None, j)

                    def step(t, ng, ahead):
                        for kind, *n in schedule(t, ng, ahead):
                            if kind == "sum":
                                sum_group(t, *n)
                            elif kind == "route":
                                route(t)
                            elif kind == "turn":
                                turn(t, *n)
                            elif kind == "up":
                                layer(t, 0, *n)
                            elif kind == "mid":
                                layer(t, 1, *n)
                            elif kind == "down":
                                down(t, *n)
                            elif kind == "bias":
                                bias(t, *n)
                            elif kind == "residual":
                                residual(t, *n)
                            elif kind == "xT":
                                xT(t, *n)

                    run(pe, step)


_INS = ["x", "src", "dst", "edge_type_8", "edge_weight", "L0_gnn_weight", "L0_ffn_Wr", "L0_ffn_br",
        "L0_ffn_W1", "L0_ffn_b1", "L0_ffn_g1", "L0_ffn_be1", "L0_ffn_m1", "L0_ffn_v1",
        "L0_ffn_W2", "L0_ffn_b2", "L0_ffn_g2", "L0_ffn_be2", "L0_ffn_m2", "L0_ffn_v2", "L0_ffn_Wo", "L0_ffn_bo"]


def kernel(**inputs):
    import numpy as np
    import concourse.bacc as bacc
    from concourse import mybir as mb
    from concourse.bass_utils import run_bass_kernel_spmd

    nc = bacc.Bacc("TRN2", target_bir_lowering=False, num_devices=1)
    arrays, args = {}, []
    for name in _INS:
        a = np.ascontiguousarray(inputs[name])
        arrays[f"in_{name}"] = a
        args.append(nc.dram_tensor(f"in_{name}", a.shape, mb.dt.from_np(a.dtype), kind="ExternalInput").ap())
    low = lower_bounds()
    arrays["in_low"] = low
    args.append(nc.dram_tensor("in_low", low.shape, mb.dt.float32, kind="ExternalInput").ap())
    args.append(nc.dram_tensor("out", (N, D), mb.dt.float32, kind="ExternalOutput").ap())
    gnn_ffn(nc, *args)
    r = run_bass_kernel_spmd(nc, [arrays], core_ids=[0])
    return r.results[0]["out"]
```
